# Optimizing a Trainium2 kernel written in Bass

```python
import numpy as np
import jax
import jax.numpy as jnp

def _softmax(x, axis=-1):
    return jax.nn.softmax(x, axis=axis)

def _gelu(x):
    return jax.nn.gelu(x, approximate=True)

def _silu(x):
    return jax.nn.silu(x)

def _sigmoid(x):
    return jax.nn.sigmoid(x)

def _layernorm(x, axis=-1, eps=1e-05):
    m = jnp.mean(x, axis=axis, keepdims=True)
    v = jnp.var(x, axis=axis, keepdims=True)
    return (x - m) / jnp.sqrt(v + eps)

def _scatter_add(tgt, idx, src, axis=0):
    return tgt.at[idx].add(src)

def _segment_sum(src, seg, n):
    return jax.ops.segment_sum(src, seg, n)
kernel_name = 'mk_adj_ffn_d1_adj_r2_facdbe'

def setup_inputs(seed: int=0):
    np.random.seed(seed)
    _w = jnp.asarray

    def _rec_inputs():
        import jax
        import jax.numpy as jnp
        _gk = jax.random.key(seed)
        x = -8.776e-05 + 1 * jax.random.normal(jax.random.fold_in(_gk, 1), (10000, 128), jnp.float32)
        _a = jax.random.bernoulli(jax.random.fold_in(_gk, 2), 0.0004, (10000, 10000))
        _a = jnp.logical_or(_a, jnp.eye(10000, dtype=bool))
        _af = _a.astype(jnp.float32)
        _af = _af * jax.random.uniform(jax.random.fold_in(_gk, 3), (10000, 10000), jnp.float32, 0.05, 1)
        adj = _af
        return (x, adj)
    x, adj = _rec_inputs()

    def _L0_gnn_setup():
        import jax, jax.numpy as jnp
        import numpy as np
        N_USER = 10000
        N_ITEM = 10000
        HID = 128
        key = jax.random.key(seed)
        k1, k2, k3, k4, k5, k6, k7 = jax.random.split(key, 7)
        scale = 1.0 / np.sqrt(HID)
        return {'user_feat': jax.random.normal(k1, (N_USER, HID), dtype=jnp.float32), 'item_feat': jax.random.normal(k2, (N_ITEM, HID), dtype=jnp.float32), 'adj': jax.random.uniform(k3, (N_USER, N_ITEM), dtype=jnp.float32), 'W_item': jax.random.uniform(k4, (HID, HID), dtype=jnp.float32, minval=-scale, maxval=scale), 'b_item': jax.random.uniform(k5, (HID,), dtype=jnp.float32, minval=-scale, maxval=scale), 'W_user': jax.random.uniform(k6, (HID, HID), dtype=jnp.float32, minval=-scale, maxval=scale), 'b_user': jax.random.uniform(k7, (HID,), dtype=jnp.float32, minval=-scale, maxval=scale)}
    _L0_gnn_all = _L0_gnn_setup()
    _L0_gnn_in = {k: v for k, v in _L0_gnn_all.items() if k in ('item_feat', 'W_item', 'b_item', 'W_user', 'b_user')}
    del _L0_gnn_all

    def _L0_ffn_setup():
        import jax, jax.numpy as jnp
        import numpy as np
        TOP_K = 2
        LN_EPS = 1e-05
        key = jax.random.key(seed)
        ks = jax.random.split(key, 8)
        B, S, D, E, H = (16, 512, 128, 8, 512)
        x = jax.random.normal(ks[0], (B, S, D), dtype=jnp.float32)
        Wr = jax.random.normal(ks[1], (D, E), dtype=jnp.float32) * 0.1
        br = jnp.zeros((E,), dtype=jnp.float32)
        ln_g = jnp.ones((E, D), dtype=jnp.float32)
        ln_b = jnp.zeros((E, D), dtype=jnp.float32)
        W1 = jax.random.normal(ks[2], (E, D, H), dtype=jnp.float32) * (1.0 / np.sqrt(D))
        b1 = jnp.zeros((E, H), dtype=jnp.float32)
        W2 = jax.random.normal(ks[3], (E, H, D), dtype=jnp.float32) * (1.0 / np.sqrt(H))
        b2 = jnp.zeros((E, D), dtype=jnp.float32)
        return {'x': x, 'Wr': Wr, 'br': br, 'ln_g': ln_g, 'ln_b': ln_b, 'W1': W1, 'b1': b1, 'W2': W2, 'b2': b2}
    _L0_ffn_all = _L0_ffn_setup()
    _L0_ffn_in = {k: v for k, v in _L0_ffn_all.items() if k in ('Wr', 'br', 'ln_g', 'ln_b', 'W1', 'b1', 'W2', 'b2')}
    del _L0_ffn_all
    return {'x': x, 'adj': adj, 'L0_gnn_item_feat': _L0_gnn_in['item_feat'], 'L0_gnn_W_item': _L0_gnn_in['W_item'], 'L0_gnn_b_item': _L0_gnn_in['b_item'], 'L0_gnn_W_user': _L0_gnn_in['W_user'], 'L0_gnn_b_user': _L0_gnn_in['b_user'], 'L0_ffn_Wr': _L0_ffn_in['Wr'], 'L0_ffn_br': _L0_ffn_in['br'], 'L0_ffn_ln_g': _L0_ffn_in['ln_g'], 'L0_ffn_ln_b': _L0_ffn_in['ln_b'], 'L0_ffn_W1': _L0_ffn_in['W1'], 'L0_ffn_b1': _L0_ffn_in['b1'], 'L0_ffn_W2': _L0_ffn_in['W2'], 'L0_ffn_b2': _L0_ffn_in['b2']}

def reference(x, adj, L0_gnn_item_feat, L0_gnn_W_item, L0_gnn_b_item, L0_gnn_W_user, L0_gnn_b_user, L0_ffn_Wr, L0_ffn_br, L0_ffn_ln_g, L0_ffn_ln_b, L0_ffn_W1, L0_ffn_b1, L0_ffn_W2, L0_ffn_b2):
    import jax
    import jax.numpy as jnp

    def _L0_gnn_ref(user_feat, item_feat, adj, W_item, b_item, W_user, b_user):
        import jax, jax.numpy as jnp
        import numpy as np
        N_USER = 10000
        N_ITEM = 10000
        HID = 128
        h = item_feat @ W_item.T + b_item
        b = user_feat @ W_user.T + b_user
        return jax.nn.relu(adj @ h + b)

    def _L0_ffn_ref(x, Wr, br, ln_g, ln_b, W1, b1, W2, b2):
        import jax, jax.numpy as jnp
        import numpy as np
        TOP_K = 2
        LN_EPS = 1e-05
        B, S, D = x.shape
        N = B * S
        xt = x.reshape(N, D)
        logits = xt @ Wr + br
        probs = jax.nn.softmax(logits, axis=-1)
        top_p, top_idx = jax.lax.top_k(probs, TOP_K)
        weights = top_p / top_p.sum(axis=-1, keepdims=True)
        mu = xt.mean(axis=-1, keepdims=True)
        var = ((xt - mu) ** 2).mean(axis=-1, keepdims=True)
        xn = (xt - mu) * jax.lax.rsqrt(var + LN_EPS)
        xe = xn[None, :, :] * ln_g[:, None, :] + ln_b[:, None, :]
        h = jax.nn.gelu(jnp.einsum('end,edh->enh', xe, W1) + b1[:, None, :], approximate=False)
        y = jnp.einsum('enh,ehd->end', h, W2) + b2[:, None, :]
        y_tok = jnp.transpose(y, (1, 0, 2))
        sel = jnp.take_along_axis(y_tok, top_idx[:, :, None], axis=1)
        out = (weights[:, :, None] * sel).sum(axis=1)
        return out.reshape(B, S, D)
    x = x + _L0_gnn_ref(_layernorm(x, axis=-1), L0_gnn_item_feat, adj, L0_gnn_W_item, L0_gnn_b_item, L0_gnn_W_user, L0_gnn_b_user)
    x = x + _L0_ffn_ref(_layernorm(x, axis=-1)[None], L0_ffn_Wr, L0_ffn_br, L0_ffn_ln_g, L0_ffn_ln_b, L0_ffn_W1, L0_ffn_b1, L0_ffn_W2, L0_ffn_b2)[0]
    return x

_drawn_inputs = setup_inputs


def setup_inputs(seed=0):
    import zlib

    import numpy as np

    out = dict(_drawn_inputs(seed))
    spreads = {'L0_ffn_br': (0.0, 0.1),
     'L0_ffn_ln_g': (1.0, 0.2),
     'L0_ffn_ln_b': (0.0, 0.1),
     'L0_ffn_b1': (0.0, 0.1),
     'L0_ffn_b2': (0.0, 0.1)}
    factors = {}
    for name, (base, spread) in spreads.items():
        noise = np.random.default_rng([zlib.crc32(name.encode()), seed]).standard_normal(out[name].shape)
        drawn = base * np.exp(spread * noise) if base else spread * noise
        out[name] = jnp.asarray(drawn.astype(out[name].dtype))
    for name, factor in factors.items():
        out[name] = (out[name] * factor).astype(out[name].dtype)
    return out
```

```python
from contextlib import ExitStack

import concourse.bass as bass
from concourse import mybir

F32 = mybir.dt.float32
U32 = mybir.dt.uint32
ALU = mybir.AluOpType
ACT = mybir.ActivationFunctionType

P = 128
BLK = 32
EPS = 1e-5
E_CONST = 2.718281828459045


def graph_moe_kernel(nc, x, adj, item_feat, W_item, b_item, W_user, b_user,
                     Wr, br, ln_g, ln_b, W1, b1, W2, b2, out):
    N, D = x.shape
    E, _, H = W1.shape
    HC = H // P
    NG = P // BLK
    KT = N // P
    GI = KT * BLK
    REM0 = N - BLK
    REM_OLD = BLK - (N - KT * P)
    NP_ = 6
    KP = KT // NP_
    J = KP * BLK
    U = 512
    R = U // BLK
    CH = -(-N // U)
    LAST = CH - 1
    U_LAST = -(-(N - LAST * U) // BLK) * BLK
    START_LAST = N - U_LAST
    NAT = 3
    TS = 2
    SMALL = 10
    assert D == P and GI * NG == KT * P and KP * NP_ == KT and NP_ % NAT == 0 and NP_ % TS == 0

    x1_dram = nc.dram_tensor("x1_rows", [CH * U, D], F32, kind="Internal").ap()
    xn3T_dram = nc.dram_tensor("xn3T_chunks", [CH, P, U], F32, kind="Internal").ap()
    wT_dram = nc.dram_tensor("route_weights", [CH, U // P * E, P], F32, kind="Internal").ap()

    with ExitStack() as ctx:
        def sb(name, shape, dt=F32):
            return ctx.enter_context(nc.sbuf_tensor(name, shape, dt))

        def sem(name):
            return ctx.enter_context(nc.semaphore(name))

        nat = sb("nat", [P, NAT, R, J])
        adjT = sb("adjT", [P, TS, KP, U])
        h_rows = sb("h_rows", [P, KT + 1, D])
        rem_nat = sb("rem_nat", [BLK, 2, R, BLK])
        rem_T = sb("rem_T", [BLK, 2, U])
        xin = sb("xin", [P, 2, U // P, D])
        xn1 = sb("xn1", [P, U // P, D])
        xnT = sb("xnT", [P, U])
        gT = sb("gT", [P, U])
        x1 = sb("x1", [P, 2, U // P, D])
        xn2 = sb("xn2", [P, U // P, D])
        xn3 = sb("xn3", [P, U // P, D])
        xn2T = sb("xn2T", [P, U])
        xn3T = sb("xn3T", [P, 2, U])
        ident = sb("ident", [P, P])
        iota_e = sb("iota_e", [P, E])
        half_neg = sb("half_neg", [P, 4])
        base_e = sb("base_e", [P, 4])
        eps4 = sb("eps4", [P, 4])
        wi_nat = sb("wi_nat", [P, D])
        wu_nat = sb("wu_nat", [P, D])
        wiT = sb("wiT", [P, D])
        wuT = sb("wuT", [P, D])
        bi_rows = sb("bi_rows", [P, D])
        br_rows = sb("br_rows", [P, E])
        bu_col = sb("bu_col", [P, 1])
        wr_sb = sb("wr_sb", [P, E])
        st = [sb(f"ln{n}_stats", [P, 4, 6]) for n in (1, 2, 3)]
        mv = [sb(f"ln{n}_mean_var", [P, 4, 2]) for n in (1, 2, 3)]
        ve = [sb(f"ln{n}_var_eps", [P, 4]) for n in (1, 2, 3)]
        rs = [sb(f"ln{n}_rstd", [P, 4]) for n in (1, 2, 3)]
        logit = sb("logit", [P, 4, E])
        top = sb("top", [P, 4, 8])
        top_i = sb("top_i", [P, 4, 8], U32)
        top_f = sb("top_f", [P, 4, 2])
        gap = sb("gap", [P, 4])
        egap = sb("egap", [P, 4])
        esum = sb("esum", [P, 4])
        pick_w = sb("pick_w", [P, 4, 2])
        oh = sb("oh", [P, 2, 4, E])
        w_rows = sb("w_rows", [P, 4, E])
        wT_sb = sb("wT_sb", [4 * E, P])
        par = sb("par", [P, P])
        parT = sb("parT", [P, P])
        b1p = sb("b1p", [P, E * HC])
        featT = adjT[:, 1, 0:2, :]
        w1_sb = nat[:, 0, :, :].rearrange("p r j -> p (r j)")[:, 0:E * H].rearrange("p (e h) -> p e h", e=E)
        w2_sb = nat[:, 1, :, :].rearrange("p r j -> p (r j)")[:, 0:E * H].rearrange("p (e c d) -> p e c d", e=E, c=HC)
        hT = adjT[:, 0, 0:2 * HC, :].rearrange("p (s c) u -> p s c u", s=2)
        outT, part = adjT[:, 0, 8, :], adjT[:, 0, 9, :]
        fin = adjT[:, 0, 10:12, :].rearrange("p s (t d) -> p s t d", d=D)
        wbc = [adjT[:, 1, 0:E, :].rearrange("p a u -> p (a u)"),
               nat[:, 2, :, :].rearrange("p r j -> p (r j)")[:, 0:E * U]]

        bank = [ctx.enter_context(nc.psum_tensor(f"bank{n}", [P, 512], F32)) for n in range(8)]
        acc = bank[0:2]
        ps_x, ps_g, ps_n2, ps_n3, ps_l, ps_w = bank[2:8]

        consts_loaded = sem("consts_loaded")
        feat_loaded = sem("feat_loaded")
        nat_loaded = [sem(f"nat_loaded{s}") for s in range(NAT)]
        rem_loaded = [sem(f"rem_loaded{s}") for s in range(2)]
        x_loaded = [sem(f"x_loaded{s}") for s in range(2)]
        passed = sem("passed")
        ident_zero = sem("ident_zero")
        par_zero = sem("par_zero")
        top_i_ready = sem("top_i_ready")
        ident_ready = sem("ident_ready")
        bases_ready = sem("bases_ready")
        wT_psum = sem("wT_psum")
        wT_ready = sem("wT_ready")
        feat_turned = sem("feat_turned")
        featT_ready = sem("featT_ready")
        h_psum = sem("h_psum")
        h_ready = sem("h_ready")
        h_zeroed = sem("h_zeroed")
        adj_turned = sem("adj_turned")
        rem_turned = sem("rem_turned")
        piece_used = sem("piece_used")
        acc_done = sem("acc_done")
        g_ready = sem("g_ready")
        g_turned = sem("g_turned")
        ln_st = [sem(f"ln{n}_st") for n in (1, 2, 3)]
        ln_mv = [sem(f"ln{n}_mv") for n in (1, 2, 3)]
        ln_ve = [sem(f"ln{n}_ve") for n in (1, 2, 3)]
        ln_rs = [sem(f"ln{n}_rs") for n in (1, 2, 3)]
        xn1_ready = sem("xn1_ready")
        xn1_turned = sem("xn1_turned")
        xnT_ready = sem("xnT_ready")
        x1_ready = sem("x1_ready")
        x1_stored = [sem(f"x1_stored{s}") for s in range(2)]
        xn2_ready = sem("xn2_ready")
        xn3_ready = sem("xn3_ready")
        xn23_turned = sem("xn23_turned")
        xn2T_ready = sem("xn2T_ready")
        xn3T_ready = sem("xn3T_ready")
        xn3T_stored = [sem(f"xn3T_stored{s}") for s in range(2)]
        logits_psum = sem("logits_psum")
        logits_ready = sem("logits_ready")
        top_ready = sem("top_ready")
        gap_ready = sem("gap_ready")
        egap_ready = sem("egap_ready")
        pick_steps = sem("pick_steps")
        w_rows_ready = sem("w_rows_ready")
        w_turned = sem("w_turned")
        wT_sb_ready = sem("wT_sb_ready")
        wT_stored = sem("wT_stored")
        w1_loaded = sem("w1_loaded")
        w2_loaded = sem("w2_loaded")
        par_turned = sem("par_turned")
        parT_ready = sem("parT_ready")
        b1_psum = sem("b1_psum")
        b1p_ready = sem("b1p_ready")
        w1g_ready = sem("w1g_ready")
        tok_loaded = [sem(f"tok_loaded{s}") for s in range(2)]
        wbc_loaded = [sem(f"wbc_loaded{s}") for s in range(2)]
        x1_loaded = [sem(f"x1_loaded{s}") for s in range(2)]
        up_psum = sem("up_psum")
        gelu_ready = sem("gelu_ready")
        y_psum = sem("y_psum")
        y_part = sem("y_part")
        out_steps = sem("out_steps")
        y_used = sem("y_used")
        out_turned = sem("out_turned")
        fin_ready = sem("fin_ready")
        out_stored = [sem(f"out_stored{s}") for s in range(2)]

        item_groups = [list(range(4 * q, min(4 * q + 4, KT))) for q in range(-(-KT // 4))]
        item_groups[-1].append(KT)
        NQ = len(item_groups)

        class At:

            def __init__(self, c, parity, before):
                self.c, self.s, self.before = c, parity, before
                self.fixed = isinstance(c, int)
                self.there = not self.fixed or 0 <= c <= LAST
                self.last = self.fixed and c == LAST

            def back(self, n):
                s = (self.s - n) % 2
                return At(self.c - n, s, self.before + (self.s - n - s) // 2)

            @property
            def n(self):
                return U_LAST if self.last else U

            def tiles(self):
                return [(t, t * P, min(P, self.n - t * P)) for t in range(-(-self.n // P))]

            def rows(self, a):
                return a[START_LAST:N, :] if self.last else self.span(a)

            def span(self, a):
                return a[self.c * U:self.c * U + U, :] if self.fixed else a[bass.ds(self.c * U, U), :]

            def own(self, a):
                return a[self.c, :, :] if self.fixed else a[bass.ds(self.c, 1), :, :].rearrange("a p n -> (a p) n")

        def chunks(eng, step, lo, lag):
            hi = LAST - 1
            for c in range(lo):
                step(At(c, c % 2, c // 2))
            with eng.Fori(0, (hi - lo) // 2) as pair:
                for s in range(2):
                    step(At(pair * 2 + (lo + s), s, pair + lo // 2))
            for c in range(hi, LAST + lag + 1):
                step(At(c, c % 2, c // 2))

        def after(eng, s, n):
            if not isinstance(n, int) or n > 0:
                eng.wait_ge(s, n)

        def wait_alone(eng, s, n):
            eng.wait_ge(s, n)
            eng.sem_inc(passed, 1)

        def load_adj(eng, k, i, ranges):
            after(eng, adj_turned, k.c * NP_ + (i - NAT + 1))
            rows = k.rows(adj)
            for g in ranges:
                eng.dma_start(nat[g * BLK:(g + 1) * BLK, i % NAT, 0:k.n // BLK, :],
                              rows[:, g * GI + i * J:g * GI + (i + 1) * J].rearrange("(r a) j -> a r j", a=BLK)
                              ).then_inc(nat_loaded[i % NAT], 16)

        def turn(pe, dst, src, k):
            for t, t0, m in k.tiles():
                ins = pe.transpose(dst[:, t0:t0 + m], src[0:m, t, :], ident[0:m, 0:m])
            return ins

        def turn_back(pe, dst, src, k):
            for t, t0, m in k.tiles():
                ins = pe.transpose(dst[0:m, t * D:(t + 1) * D], src[:, t0:t0 + m], ident[:])
            return ins

        def move_rows(eng, k, dst_of, src_of, whole, s, per_chunk):
            if not k.last:
                eng.dma_start(*whole).then_inc(s, 16)
            else:
                for t, t0, m in k.tiles():
                    eng.dma_start(dst_of(t, t0, m), src_of(t, t0, m)).then_inc(s, 16)

        LT = len(At(LAST, 0, 0).tiles())

        def moved(k):
            return (k.before + (LT if k.last else 1)) * 16

        block = ctx.enter_context(nc.Block())

        @block.sync
        def _(sp):
            for g in range(NG):
                sp.dma_start(h_rows[g * BLK:(g + 1) * BLK, 0:KT, :],
                             item_feat[g * GI:(g + 1) * GI, :].rearrange("(k j) f -> j k f", j=BLK)
                             ).then_inc(feat_loaded, 16)
            sp.dma_start(h_rows[0:BLK, KT, :], item_feat[REM0:N, :]).then_inc(feat_loaded, 16)
            small = [(wi_nat[:], W_item), (wu_nat[:], W_user),
                     (bi_rows[:], b_item.rearrange("(a d) -> a d", a=1).broadcast_to([P, D])),
                     (br_rows[:], br.rearrange("(a d) -> a d", a=1).broadcast_to([P, E])),
                     (bu_col[:], b_user.rearrange("(d a) -> d a", a=1)), (wr_sb[:], Wr),
                     (par[0:E * HC, :], b1.rearrange("e (c p) -> (e c) p", p=P)),
                     (par[32:32 + E, :], ln_g), (par[64:64 + E, :], ln_b), (par[96:96 + E, :], b2)]
            assert len(small) == SMALL
            sp.wait_ge(par_zero, 1)
            for dst, src in small:
                sp.dma_start(dst, src).then_inc(consts_loaded, 16)

            def step(k):
                k2, k3, k4 = k.back(2), k.back(3), k.back(4)
                for i in range(NP_):
                    if k.there:
                        load_adj(sp, k, i, (0, 1))
                    if i == 1 and k.there:
                        after(sp, x1_ready, k.c - 1)
                        xr = k.rows(x)
                        move_rows(sp, k, lambda t, t0, m: xin[0:m, k.s, t, :], lambda t, t0, m: xr[t0:t0 + m, :],
                                  (xin[:, k.s, :, :], xr.rearrange("(t p) d -> p t d", p=P) if not k.last else None),
                                  x_loaded[k.s], 16)
                        after(sp, rem_turned, k.c - 1)
                        sp.dma_start(rem_nat[:, k.s, 0:k.n // BLK, :],
                                     k.rows(adj)[:, REM0:N].rearrange("(r a) j -> a r j", a=BLK)
                                     ).then_inc(rem_loaded[k.s], 16)
                    if i == 1 and k3.there:
                        sp.wait_ge(xn3T_ready, k3.c + 1)
                        sp.dma_start(k3.own(xn3T_dram)[:, 0:k3.n], xn3T[:, k3.s, 0:k3.n]).then_inc(xn3T_stored[k3.s], 16)
                    if i == 2 and k2.there:
                        sp.wait_ge(x1_ready, k2.c + 1)
                        xr2 = k2.span(x1_dram)
                        move_rows(sp, k2, lambda t, t0, m: xr2[t0:t0 + m, :], lambda t, t0, m: x1[0:m, k2.s, t, :],
                                  (xr2.rearrange("(t p) d -> p t d", p=P), x1[:, k2.s, :, :]), x1_stored[k2.s], 16)
                    if i == 2 and k4.there:
                        sp.wait_ge(wT_sb_ready, k4.c + 1)
                        m = len(k4.tiles()) * E
                        sp.dma_start(k4.own(wT_dram)[0:m, :], wT_sb[0:m, :]).then_inc(wT_stored, 16)

            chunks(sp, step, 6, 4)

            sp.wait_ge(adj_turned, CH * NP_)
            sp.dma_start(w1_sb, W1.rearrange("e d h -> d e h")).then_inc(w1_loaded, 16)
            for e in range(E):
                sp.dma_start(w2_sb[:, e, :, :], W2[e, :, :].rearrange("(c p) d -> p c d", p=P)).then_inc(w2_loaded, 16)
            sp.wait_ge(acc_done, CH)
            for s in range(2):
                sp.wait_ge(xn3T_stored[s], 16 * (CH // 2))
                sp.wait_ge(x1_stored[s], moved(At(CH - 2 + s, s, CH // 2 - 1)))
            sp.wait_ge(wT_stored, 16 * CH)

            def tokens(k):
                if k.there:
                    after(sp, fin_ready, k.c - 1)
                    sp.dma_start(xn3T[:, k.s, 0:k.n], k.own(xn3T_dram)[:, 0:k.n]).then_inc(tok_loaded[k.s], 16)
                    w = len(k.tiles()) * E
                    src = wT_dram[k.c:k.c + 1, 0:w, :] if k.fixed else wT_dram[bass.ds(k.c, 1), 0:w, :]
                    sp.dma_start(wbc[k.s][:, 0:w * P], src.rearrange("a p u -> a (p u)").broadcast_to([P, w * P])
                                 ).then_inc(wbc_loaded[k.s], 16)
                    xr = k.span(x1_dram)
                    move_rows(sp, k, lambda t, t0, m: x1[0:m, k.s, t, :], lambda t, t0, m: xr[t0:t0 + m, :],
                              (x1[:, k.s, :, :], xr.rearrange("(t p) d -> p t d", p=P)), x1_loaded[k.s], 16)
                b = k.back(2)
                if b.there:
                    sp.wait_ge(fin_ready, b.c + 1)
                    o = b.rows(out)
                    skip = LAST * U - START_LAST
                    move_rows(sp, b, lambda t, t0, m: o[t0 + (skip if t == 0 else 0):t0 + m, :],
                              lambda t, t0, m: fin[(skip if t == 0 else 0):m, b.s, t, :],
                              (o.rearrange("(t p) d -> p t d", p=P) if not b.last else None, fin[:, b.s, :, :]),
                              out_stored[b.s], 16)

            chunks(sp, tokens, 4, 2)
            for s in range(2):
                sp.wait_ge(out_stored[s], moved(At(CH - 2 + s, s, CH // 2 - 1)))

        @block.scalar
        def _(act):
            for i in range(NAT):
                load_adj(act, At(0, 0, 0), i, (2, 3))
            act.wait_ge(wT_psum, 2)
            act.activation(wiT[:], ps_x[:, 0:D], ACT.Copy).then_inc(wT_ready, 1)
            act.activation(wuT[:], ps_x[:, D:2 * D], ACT.Copy).then_inc(wT_ready, 1)
            act.wait_ge(par_turned, 1)
            act.activation(parT[:], ps_g[:, 0:P], ACT.Copy).then_inc(parT_ready, 1)
            for q in range(NQ):
                act.wait_ge(feat_turned, q + 1)
                after(act, h_psum, q - 1)
                w = P * len(item_groups[q]) - (P - BLK) * (q == NQ - 1)
                act.activation(featT[:, q % 2, 0:w], bank[4 + q % 2][:, 0:w], ACT.Copy).then_inc(featT_ready, 1)

            def step(k):
                k1, k2, k3 = k.back(1), k.back(2), k.back(3)
                for i in range(NP_):
                    if k.there and not (k.fixed and k.c == 0 and i < NAT):
                        load_adj(act, k, i, (2, 3))
                    if i == 4 and k1.there:
                        act.wait_ge(acc_done, k1.c + 1)
                        after(act, g_turned, k1.c)
                        act.activation(gT[:, 0:k1.n], acc[k1.s][:, 0:k1.n], ACT.Relu,
                                       bias=bu_col[:, 0:1]).then_inc(g_ready, 1)
                    if i == 5 and k.there:
                        act.wait_ge(xn1_turned, k.c + 1)
                        after(act, acc_done, k.c)
                        act.activation(xnT[:, 0:k.n], ps_x[:, 0:k.n], ACT.Copy).then_inc(xnT_ready, 1)
                    if i == 5 and k2.there:
                        act.wait_ge(xn23_turned, k2.c + 1)
                        after(act, logits_psum, k2.c)
                        act.activation(xn2T[:, 0:k2.n], ps_n2[:, 0:k2.n], ACT.Copy).then_inc(xn2T_ready, 1)
                        after(act, xn3T_stored[k2.s], k2.before * 16)
                        act.activation(xn3T[:, k2.s, 0:k2.n], ps_n3[:, 0:k2.n], ACT.Copy).then_inc(xn3T_ready, 1)
                    if i == 5 and k3.there:
                        m = len(k3.tiles()) * E
                        act.wait_ge(w_turned, k3.c + 1)
                        after(act, wT_stored, k3.c * 16)
                        act.activation(wT_sb[0:m, :], ps_w[0:m, 0:P], ACT.Copy).then_inc(wT_sb_ready, 1)

            chunks(act, step, 6, 3)
            act.wait_ge(b1p_ready, 1)

            def tokens(k):
                for e in range(E):
                    after(act, y_psum, k.c * E + (e - 1))
                    for m in range(HC):
                        act.wait_ge(up_psum, k.c * (E * HC) + (e * HC + m + 1))
                        act.activation(hT[:, e % 2, m, 0:k.n], bank[m][:, 0:k.n], ACT.Gelu,
                                       bias=b1p[:, e * HC + m:e * HC + m + 1]).then_inc(gelu_ready, 1)

            chunks(act, tokens, 2, 0)

        @block.gpsimd
        def _(pool):
            pool.memset(ident[:], 0.0).then_inc(ident_zero, 1)
            pool.wait_ge(ident_zero, 1)
            pool.affine_select(out=ident[:], in_=ident[:], compare_op=ALU.not_equal, fill=1.0, base=0,
                               pattern=[[-1, P]], channel_multiplier=1).then_inc(ident_ready, 1)
            pool.memset(par[:], 0.0).then_inc(par_zero, 1)
            pool.iota(iota_e[:], [[1, E]], base=0, channel_multiplier=0,
                      allow_small_or_imprecise_dtypes=True).then_inc(bases_ready, 1)
            pool.memset(half_neg[:], -0.5).then_inc(bases_ready, 1)
            pool.memset(base_e[:], E_CONST).then_inc(bases_ready, 1)
            pool.memset(eps4[:], EPS).then_inc(bases_ready, 1)
            pool.wait_ge(bases_ready, 4)

            def rstd(n, k):
                T = len(k.tiles())
                pool.wait_ge(ln_mv[n], k.c + 1)
                pool.tensor_tensor(ve[n][:, 0:T], mv[n][:, 0:T, 1], eps4[:, 0:T], ALU.add).then_inc(ln_ve[n], 1)
                pool.wait_ge(ln_ve[n], k.c + 1)
                pool.tensor_tensor(rs[n][:, 0:T], ve[n][:, 0:T], half_neg[:, 0:T], ALU.pow).then_inc(ln_rs[n], 1)

            def step(k):
                k1, k2 = k.back(1), k.back(2)
                if k.there:
                    rstd(0, k)
                if k1.there:
                    rstd(1, k1)
                    rstd(2, k1)
                if k2.there:
                    T = len(k2.tiles())
                    pool.wait_ge(gap_ready, k2.c + 1)
                    pool.tensor_tensor(egap[:, 0:T], base_e[:, 0:T], gap[:, 0:T], ALU.pow).then_inc(egap_ready, 1)

            chunks(pool, step, 6, 2)

        @block.tensor
        def _(pe):
            pe.wait_ge(ident_ready, 1)
            pe.wait_ge(consts_loaded, 16 * SMALL)
            pe.transpose(ps_x[:, 0:D], wi_nat[:], ident[:]).then_inc(wT_psum, 1)
            pe.transpose(ps_x[:, D:2 * D], wu_nat[:], ident[:]).then_inc(wT_psum, 1)
            pe.transpose(ps_g[:, 0:P], par[:], ident[:]).then_inc(par_turned, 1)

            pe.wait_ge(feat_loaded, 16 * (NG + 1))
            pe.wait_ge(wT_ready, 2)
            for q in range(NQ + 1):
                if q < NQ:
                    after(pe, featT_ready, q - 1)
                    for n, t in enumerate(item_groups[q]):
                        m = BLK if t == KT else P
                        ins = pe.transpose(bank[4 + q % 2][:, n * P:n * P + m], h_rows[0:m, t, :], ident[0:m, 0:m])
                    ins.then_inc(feat_turned, 1)
                if q > 0:
                    b = q - 1
                    pe.wait_ge(featT_ready, b + 1)
                    after(pe, h_ready, b - 1)
                    for n, t in enumerate(item_groups[b]):
                        m = BLK if t == KT else P
                        ins = pe.matmul(bank[6 + b % 2][0:m, n * P:(n + 1) * P], featT[:, b % 2, n * P:n * P + m],
                                        wiT[:], start=True, stop=True)
                    ins.then_inc(h_psum, 1)
            pe.wait_ge(h_zeroed, 1)

            def step(k):
                k1, k2 = k.back(1), k.back(2)
                for i in range(NP_):
                    if k.there:
                        if i == 0:
                            after(pe, g_ready, k.c - 1)
                        pe.wait_ge(adj_turned, k.c * NP_ + (i + 1))
                        for j in range(KP):
                            ins = pe.matmul(acc[k.s][:, 0:k.n], h_rows[:, i * KP + j, :], adjT[:, i % TS, j, 0:k.n],
                                            start=(i == 0 and j == 0), stop=False)
                        ins.then_inc(piece_used, 1)
                    if i == 0 and k.there:
                        pe.wait_ge(xn1_ready, k.c + 1)
                        after(pe, xnT_ready, k.c)
                        turn(pe, ps_x, xn1, k).then_inc(xn1_turned, 1)
                    if i == 1 and k1.there:
                        pe.wait_ge(g_ready, k1.c + 1)
                        after(pe, x1_ready, k1.c)
                        turn_back(pe, ps_g, gT, k1).then_inc(g_turned, 1)
                    if i == 2 and k2.there:
                        pe.wait_ge(xn2T_ready, k2.c + 1)
                        after(pe, logits_ready, k2.c)
                        for t, t0, m in k2.tiles():
                            ins = pe.matmul(ps_l[0:m, t * E:(t + 1) * E], xn2T[:, t0:t0 + m], wr_sb[:],
                                            start=True, stop=True)
                        ins.then_inc(logits_psum, 1)
                    if i == 4 and k.there:
                        pe.wait_ge(xnT_ready, k.c + 1)
                        pe.matmul(acc[k.s][:, 0:k.n], wuT[:], xnT[:, 0:k.n], start=False, stop=False)
                    if i == 5 and k1.there:
                        pe.wait_ge(xn3_ready, k1.c + 1)
                        after(pe, xn3T_ready, k1.c)
                        turn(pe, ps_n2, xn2, k1)
                        turn(pe, ps_n3, xn3, k1).then_inc(xn23_turned, 1)
                    if i == 5 and k2.there:
                        T = len(k2.tiles())
                        pe.wait_ge(w_rows_ready, k2.c + 1)
                        after(pe, wT_sb_ready, k2.c)
                        pe.transpose(ps_w[0:T * E, 0:P], w_rows[:, 0:T, :].rearrange("p t e -> p (t e)"), ident[:]
                                     ).then_inc(w_turned, 1)
                if k.there:
                    pe.wait_ge(rem_turned, k.c + 1)
                    pe.matmul(acc[k.s][:, 0:k.n], h_rows[0:BLK, KT, :], rem_T[:, k.s, 0:k.n],
                              start=False, stop=True).then_inc(acc_done, 1)

            chunks(pe, step, 6, 2)

            pe.wait_ge(w1_loaded, 16)
            pe.wait_ge(wT_sb_ready, CH)
            for e in range(E):
                for m in range(HC):
                    ins = pe.matmul(ps_w[:, e * HC + m:e * HC + m + 1], w1_sb[:, e, m * P:(m + 1) * P],
                                    parT[:, 64 + e:65 + e], start=True, stop=True)
            ins.then_inc(b1_psum, 1)
            pe.wait_ge(w1g_ready, E)
            pe.wait_ge(w2_loaded, 16 * E)
            pe.wait_ge(g_ready, CH)
            pe.wait_ge(x1_ready, CH)
            pe.wait_ge(xn3T_ready, CH)
            pe.wait_ge(logits_ready, CH)

            def up(k, e):
                if e == 0:
                    pe.wait_ge(tok_loaded[k.s], (k.before + 1) * 16)
                for m in range(HC):
                    after(pe, gelu_ready, k.c * (E * HC) + (e * HC + m - HC + 1))
                    pe.matmul(bank[m][:, 0:k.n], w1_sb[:, e, m * P:(m + 1) * P], xn3T[:, k.s, 0:k.n],
                              start=True, stop=True).then_inc(up_psum, 1)

            def tokens(k):
                if k.fixed and k.c == 0:
                    up(k, 0)
                b = k.back(1)
                for e in range(E):
                    if k.there:
                        if e + 1 < E:
                            up(k, e + 1)
                        elif not k.last:
                            up(k.back(-1), 0)
                        after(pe, y_used, k.c * E + (e - 1))
                        for m in range(HC):
                            pe.wait_ge(gelu_ready, k.c * (E * HC) + (e * HC + m + 1))
                            ins = pe.matmul((ps_n2, ps_n3)[e % 2][:, 0:k.n], w2_sb[:, e, m, :], hT[:, e % 2, m, 0:k.n],
                                            start=(m == 0), stop=(m == HC - 1))
                        ins.then_inc(y_psum, 1)
                    if e == 1 and b.there:
                        pe.wait_ge(out_steps, b.c * (E - 1) + (E - 1))
                        after(pe, fin_ready, b.c)
                        turn_back(pe, ps_l, outT, b).then_inc(out_turned, 1)

            chunks(pe, tokens, 2, 1)

        @block.vector
        def _(dve):
            dve.wait_ge(consts_loaded, 16 * SMALL)
            for q in range(NQ):
                dve.wait_ge(h_psum, q + 1)
                for n, t in enumerate(item_groups[q]):
                    if t == KT:
                        dve.tensor_tensor(h_rows[0:BLK, t, :], bank[6 + q % 2][0:BLK, n * P:(n + 1) * P],
                                          bi_rows[0:BLK, :], ALU.add).then_inc(h_ready, 1)
                full = [t for t in item_groups[q] if t < KT]
                w = len(full)
                ins = dve.tensor_tensor(h_rows[:, full[0]:full[0] + w, :],
                                        bank[6 + q % 2][:, 0:w * P].rearrange("p (k d) -> p k d", d=D),
                                        bi_rows[:].unsqueeze(1).to_broadcast([P, w, D]), ALU.add)
                ins.then_inc(h_ready, 1)
            dve.wait_ge(h_ready, NQ + 1)
            dve.memset(h_rows[0:REM_OLD, KT, :], 0.0).then_inc(h_zeroed, 1)

            def stats(n, src, k):
                after(dve, ln_rs[n], k.c)
                for t, t0, m in k.tiles():
                    ins = dve.bn_stats(st[n][0:m, t, :], src[0:m, t, :])
                ins.then_inc(ln_st[n], 1)

            def aggregate(n, k):
                wait_alone(dve, ln_st[n], k.c + 1)
                for t, t0, m in k.tiles():
                    ins = dve.bn_aggr(mv[n][0:m, t, :], st[n][0:m, t, :])
                ins.then_inc(ln_mv[n], 1)

            def normalise(n, dst, src, k, done):
                dve.wait_ge(ln_rs[n], k.c + 1)
                for t, t0, m in k.tiles():
                    ins = dve.tensor_scalar(dst[0:m, t, :], src[0:m, t, :], mv[n][0:m, t, 0:1], rs[n][0:m, t:t + 1],
                                            ALU.subtract, ALU.mult)
                ins.then_inc(done, 1)

            def step(k):
                k1, k2 = k.back(1), k.back(2)
                for i in range(NP_):
                    if k.there:
                        dve.wait_ge(nat_loaded[i % NAT], (k.c * (NP_ // NAT) + (i // NAT + 1)) * (16 * NG))
                        after(dve, piece_used, k.c * NP_ + (i - TS + 1))
                        r = k.n // BLK
                        dve.transpose(adjT[:, i % TS, :, 0:k.n].rearrange("p k (r a) -> p r k a", a=BLK),
                                      nat[:, i % NAT, 0:r, :].rearrange("p r (k j) -> p r k j", j=BLK)
                                      ).then_inc(adj_turned, 1)
                    if i == 0 and k.there:
                        xk = xin[:, k.s, :, :]
                        dve.wait_ge(x_loaded[k.s], moved(k))
                        stats(0, xk, k)
                        aggregate(0, k)
                    if i == 1 and k.there:
                        after(dve, xn1_turned, k.c)
                        normalise(0, xn1, xin[:, k.s, :, :], k, xn1_ready)
                        dve.wait_ge(rem_loaded[k.s], (k.before + 1) * 16)
                        after(dve, acc_done, k.c - 1)
                        dve.transpose(rem_T[:, k.s, 0:k.n], rem_nat[:, k.s, 0:k.n // BLK, :].rearrange("p r j -> p (r j)")
                                      ).then_inc(rem_turned, 1)
                    if i == 3 and k1.there:
                        dve.wait_ge(g_turned, k1.c + 1)
                        after(dve, x1_stored[k1.s], k1.before * 16)
                        for t, t0, m in k1.tiles():
                            ins = dve.tensor_tensor(x1[0:m, k1.s, t, :], ps_g[0:m, t * D:(t + 1) * D],
                                                    xin[0:m, k1.s, t, :], ALU.add)
                        ins.then_inc(x1_ready, 1)
                        dve.wait_ge(x1_ready, k1.c + 1)
                        stats(1, x1[:, k1.s, :, :], k1)
                        aggregate(1, k1)
                    if i == 4 and k1.there:
                        after(dve, xn23_turned, k1.c)
                        normalise(1, xn2, x1[:, k1.s, :, :], k1, xn2_ready)
                        dve.wait_ge(xn2_ready, k1.c + 1)
                        stats(2, xn2, k1)
                        aggregate(2, k1)
                    if i == 4 and k2.there:
                        route_top(k2)
                    if i == 5 and k1.there:
                        normalise(2, xn3, xn2, k1, xn3_ready)
                    if i == 5 and k2.there:
                        route_weights(k2)

            def route_top(k):
                T, c = len(k.tiles()), k.c
                dve.wait_ge(logits_psum, c + 1)
                for t, t0, m in k.tiles():
                    ins = dve.tensor_tensor(logit[0:m, t, :], ps_l[0:m, t * E:(t + 1) * E], br_rows[0:m, :], ALU.add)
                ins.then_inc(logits_ready, 1)
                wait_alone(dve, logits_ready, c + 1)
                for t, t0, m in k.tiles():
                    ins = dve.max(top[0:m, t, :], logit[0:m, t, :])
                ins.then_inc(top_ready, 1)
                wait_alone(dve, top_ready, c + 1)
                for t, t0, m in k.tiles():
                    ins = dve.max_index(top_i[0:m, t, :], top[0:m, t, :], logit[0:m, t, :])
                ins.then_inc(top_i_ready, 1)
                dve.wait_ge(top_i_ready, c + 1)
                dve.tensor_copy(top_f[:, 0:T, :], top_i[:, 0:T, 0:2])
                dve.tensor_tensor(gap[:, 0:T], top[:, 0:T, 1], top[:, 0:T, 0], ALU.subtract).then_inc(gap_ready, 1)

            def route_weights(k):
                T, c = len(k.tiles()), k.c
                dve.wait_ge(egap_ready, c + 1)
                dve.tensor_scalar(esum[:, 0:T], egap[:, 0:T], 1.0, None, ALU.add).then_inc(pick_steps, 1)
                dve.wait_ge(pick_steps, c * 4 + 1)
                dve.reciprocal(pick_w[:, 0:T, 0], esum[:, 0:T]).then_inc(pick_steps, 1)
                dve.wait_ge(pick_steps, c * 4 + 2)
                dve.tensor_tensor(pick_w[:, 0:T, 1], egap[:, 0:T], pick_w[:, 0:T, 0], ALU.mult).then_inc(pick_steps, 1)
                dve.wait_ge(pick_steps, c * 4 + 3)
                for t in range(T):
                    for n in range(2):
                        ins = dve.tensor_scalar(oh[:, n, t, :], iota_e[:], top_f[:, t, n:n + 1], pick_w[:, t, n:n + 1],
                                                ALU.is_equal, ALU.mult)
                ins.then_inc(pick_steps, 1)
                dve.wait_ge(pick_steps, c * 4 + 4)
                after(dve, w_turned, c)
                dve.tensor_tensor(w_rows[:, 0:T, :], oh[:, 0, 0:T, :], oh[:, 1, 0:T, :], ALU.add).then_inc(w_rows_ready, 1)

            chunks(dve, step, 6, 2)

            dve.wait_ge(parT_ready, 1)
            dve.wait_ge(b1_psum, 1)
            dve.tensor_tensor(b1p[:], ps_w[:, 0:E * HC], parT[:, 0:E * HC], ALU.add).then_inc(b1p_ready, 1)
            for e in range(E):
                dve.tensor_scalar(w1_sb[:, e, :], w1_sb[:, e, :], parT[:, 32 + e:33 + e], None, ALU.mult
                                  ).then_inc(w1g_ready, 1)

            def tokens(k):
                b = k.back(1)
                for e in range(E):
                    if k.there:
                        if e == 0:
                            dve.wait_ge(wbc_loaded[k.s], (k.before + 1) * 16)
                            after(dve, out_turned, k.c)
                        dve.wait_ge(y_psum, k.c * E + (e + 1))
                        T = k.n // P
                        y = (ps_n2, ps_n3)[e % 2]
                        w = wbc[k.s][:, 0:len(k.tiles()) * E * P].rearrange("p (t e u) -> p t e u", e=E, u=P)
                        dst = outT if e == 0 else part
                        if e > 0:
                            after(dve, out_steps, k.c * (E - 1) + (e - 1))
                        parts = [(0, T, P)] + [(T, T + 1, k.n - T * P)] * (k.n > T * P)
                        for lo_t, hi_t, m in parts:
                            cols = slice(lo_t * P, lo_t * P + (hi_t - lo_t) * m)
                            ins = dve.scalar_tensor_tensor(
                                out=dst[:, cols].rearrange("p (t u) -> p t u", u=m),
                                in0=y[:, cols].rearrange("p (t u) -> p t u", u=m), scalar=parT[:, 96 + e:97 + e],
                                in1=w[:, lo_t:hi_t, e, 0:m], op0=ALU.add, op1=ALU.mult)
                        ins.then_inc(y_used, 1)
                        dve.wait_ge(y_used, k.c * E + (e + 1))
                        if e > 0:
                            dve.tensor_tensor(outT[:, 0:k.n], outT[:, 0:k.n], part[:, 0:k.n], ALU.add).then_inc(out_steps, 1)
                    if e == 2 and b.there:
                        dve.wait_ge(out_turned, b.c + 1)
                        dve.wait_ge(x1_loaded[b.s], moved(b))
                        after(dve, out_stored[b.s], b.before * 16)
                        for t, t0, m in b.tiles():
                            ins = dve.tensor_tensor(fin[0:m, b.s, t, :], ps_l[0:m, t * D:(t + 1) * D],
                                                    x1[0:m, b.s, t, :], ALU.add)
                        ins.then_inc(fin_ready, 1)

            chunks(dve, tokens, 4, 1)


_INS = ['x', 'adj', 'L0_gnn_item_feat', 'L0_gnn_W_item', 'L0_gnn_b_item', 'L0_gnn_W_user', 'L0_gnn_b_user',
        'L0_ffn_Wr', 'L0_ffn_br', 'L0_ffn_ln_g', 'L0_ffn_ln_b', 'L0_ffn_W1', 'L0_ffn_b1', 'L0_ffn_W2', 'L0_ffn_b2']


def kernel(**inputs):
    import numpy as np
    from concourse import bacc
    from concourse.bass_utils import run_bass_kernel_spmd

    nc = bacc.Bacc("TRN2", target_bir_lowering=False, num_devices=1)
    arrays, args = {}, []
    for name in _INS:
        a = np.ascontiguousarray(inputs[name])
        arrays["in_" + name] = a
        args.append(nc.dram_tensor("in_" + name, a.shape, mybir.dt.from_np(a.dtype), kind="ExternalInput").ap())
    res = nc.dram_tensor("out_rows", list(arrays["in_x"].shape), F32, kind="ExternalOutput").ap()
    graph_moe_kernel(nc, *args, res)
    r = run_bass_kernel_spmd(nc, [arrays], core_ids=[0])
    return r.results[0]["out_rows"]
```

```python
from contextlib import ExitStack

import concourse.bass as bass
from concourse import mybir

F32 = mybir.dt.float32
U32 = mybir.dt.uint32
BF16 = mybir.dt.bfloat16
AX = mybir.AxisListType
ALU = mybir.AluOpType
ACT = mybir.ActivationFunctionType

P = 128
BLK = 32
EPS = 1e-5
E_CONST = 2.718281828459045


def graph_moe_kernel(nc, x, adj, item_feat, W_item, b_item, W_user, b_user,
                     Wr, br, ln_g, ln_b, W1, b1, W2, b2, out):
    N, D = x.shape
    E, _, H = W1.shape
    HC = H // P
    NG = P // BLK
    KT = N // P
    GI = KT * BLK
    REM0 = N - BLK
    REM_OLD = BLK - (N - KT * P)
    NP_ = 6
    KP = KT // NP_
    J = KP * BLK
    U = 512
    R = U // BLK
    CH = -(-N // U)
    LAST = CH - 1
    U_LAST = -(-(N - LAST * U) // BLK) * BLK
    START_LAST = N - U_LAST
    NAT = 3
    TS = 2
    SMALL = 10
    assert D == P and GI * NG == KT * P and KP * NP_ == KT and NP_ % NAT == 0 and NP_ % TS == 0

    K = 2
    ROW = D + 1
    SLOTS = (LAST * U + U_LAST) * K
    CAP = CH * U + U
    NT = (SLOTS + E * (U - 1)) // U
    NT += NT % 2
    PLACES = CH * U
    NOWHERE = 1 << 20
    x1_dram = nc.dram_tensor("x1_rows", [CH * U, D], F32, kind="Internal").ap()
    region_dram = nc.dram_tensor("expert_regions", [E * CAP + U, ROW], F32, kind="Internal").ap()
    picks_dram = nc.dram_tensor("pick_results", [K * PLACES, D], F32, kind="Internal").ap()

    with ExitStack() as ctx:
        def sb(name, shape, dt=F32):
            return ctx.enter_context(nc.sbuf_tensor(name, shape, dt))

        def sem(name):
            return ctx.enter_context(nc.semaphore(name))

        nat = sb("nat", [P, NAT, R, J])
        adjT = sb("adjT", [P, TS, KP, U])
        h_rows = sb("h_rows", [P, KT + 1, D])
        rem_nat = sb("rem_nat", [BLK, R, BLK])
        rem_T = sb("rem_T", [BLK, U])
        xin = sb("xin", [P, 2, U // P, D])
        xn1 = sb("xn1", [P, U // P, D])
        xnT = sb("xnT", [P, U])
        gT = sb("gT", [P, U])
        x1 = sb("x1", [P, 2, U // P, D])
        xn2 = sb("xn2", [P, U // P, D])
        rows = sb("rows", [P, 2, U // P, K, ROW])
        xn2T = sb("xn2T", [P, U])
        ident = sb("ident", [P, P])
        iota_e = sb("iota_e", [P, E])
        half_neg = sb("half_neg", [P, 4])
        base_e = sb("base_e", [P, 4])
        eps4 = sb("eps4", [P, 4])
        wiT = sb("wiT", [P, D])
        wuT = sb("wuT", [P, D])
        bi_rows = sb("bi_rows", [P, D])
        br_rows = sb("br_rows", [P, E])
        bu_col = sb("bu_col", [P, 1])
        wr_sb = sb("wr_sb", [P, E])
        st = [sb(f"ln{n}_stats", [P, 4, 6]) for n in (1, 2, 3)]
        mv = [sb(f"ln{n}_mean_var", [P, 4, 2]) for n in (1, 2, 3)]
        ve = [sb(f"ln{n}_var_eps", [P, 4]) for n in (1, 2, 3)]
        rs = [sb(f"ln{n}_rstd", [P, 4]) for n in (1, 2, 3)]
        logit = sb("logit", [P, 4, E])
        top = sb("top", [P, 4, 8])
        top_i = sb("top_i", [P, 4, 8], U32)
        top_f = sb("top_f", [P, 4, 2])
        gap = sb("gap", [P, 4])
        egap = sb("egap", [P, 4])
        esum = sb("esum", [P, 4])
        pick_w = sb("pick_w", [P, 4, 2])
        is_pick = sb("is_pick", [P, K, 4, E])
        mask = sb("mask", [P, 4, E], BF16)
        before_me = sb("before_me", [P, P], BF16)
        ones = sb("ones", [P, P], BF16)
        region_end = sb("region_end", [P, E])
        pos = sb("pos", [P, 4, E])
        pos_pick = sb("pos_pick", [P, K, 4, E])
        dest_f = sb("dest_f", [P, K, 4])
        dest = sb("dest", [P, 2, K * 4], U32)
        place_f = sb("place_f", [P, K, 4])
        w_all = sb("w_all", [P, CH * 4 * K])
        w_chunk = sb("w_chunk", [P, 2, 4 * K])
        count = sb("count", [1, E])
        steps_512 = sb("steps_512", [1, CH + 1])
        n_tiles = sb("n_tiles", [1, E])
        upto = sb("upto", [1, E, E])
        upto_n = sb("upto_n", [1, E, E])
        last_tile = sb("last_tile", [1, E])
        tile_no = sb("tile_no", [1, NT])
        tab_past = sb("tab_past", [1, NT])
        tab_n = sb("tab_n", [1, NT])
        tab_rel = sb("tab_rel", [1, NT])
        tab_rowf = sb("tab_rowf", [1, NT])
        tab_row = sb("tab_row", [1, NT], U32)
        tab_e = sb("tab_e", [1, NT], U32)
        end_u = sb("end_u", [1, E], U32)
        place_now = sb("place_now", [P, 2, 4], U32)
        b1s = sb("b1s", [P, 2, HC])
        b2s = sb("b2s", [P, 2, 1])
        parT = sb("parT", [P, P])
        wi_nat, wu_nat, par = (adjT[:, 1, 2, n * P:(n + 1) * P] for n in range(3))
        fill = rows[:, 0, :, 0, :]
        featT = adjT[:, 1, 0:2, :]
        w1_sb = nat[:, 0, :, :].rearrange("p r j -> p (r j)")[:, 0:E * H].rearrange("p (e h) -> p e h", e=E)
        w2_sb = nat[:, 1, :, :].rearrange("p r j -> p (r j)")[:, 0:E * H].rearrange("p (e c d) -> p e c d", e=E, c=HC)
        hT = adjT[:, 0, 0:2 * HC, :].rearrange("p (s c) u -> p s c u", s=2)
        xT = adjT[:, 0, 8:10, :]
        yT = adjT[:, 0, 10, :]
        y_rows = adjT[:, 0, 11:13, :].rearrange("p s (t d) -> p s t d", d=D)
        spare = nat[:, 2, :, :].rearrange("p r j -> p (r j)")
        w1s = spare[:, 0:2 * H].rearrange("p (s h) -> p s h", s=2)
        w2s = spare[:, 2 * H:4 * H].rearrange("p (s c d) -> p s c d", s=2, c=HC)
        xs = spare[:, 4 * H:4 * H + 8 * ROW].rearrange("p (s t d) -> p s t d", s=2, t=4)
        over = spare[0:1, 4000:4000 + E * (CH + 1)].rearrange("p (e n) -> p e n", e=E)
        past = spare[0:1, 4400:4400 + NT * E].rearrange("p (n e) -> p n e", e=E)
        past_n = spare[0:1, 4800:4800 + NT * E].rearrange("p (n e) -> p n e", e=E)
        places = spare[:, 5200:5200 + NT * 4].bitcast(U32)
        cols = spare[:, 5400:5400 + E * (HC + 1)].rearrange("p (e c) -> p e c", e=E)
        picks = adjT[:, 1, 0:2 * K, :].rearrange("p (s n) (t d) -> p s n t d", s=2, d=D)
        fin = adjT[:, 1, 4:6, :].rearrange("p s (t d) -> p s t d", d=D)

        bank = [ctx.enter_context(nc.psum_tensor(f"bank{n}", [P, 512], F32)) for n in range(8)]
        acc = bank[0:2]
        ps_x, ps_g, ps_n2, ps_n3, ps_l, ps_w = bank[2:8]

        consts_loaded = sem("consts_loaded")
        feat_loaded = sem("feat_loaded")
        nat_loaded = [sem(f"nat_loaded{s}") for s in range(NAT)]
        rem_loaded = sem("rem_loaded")
        x_loaded = [sem(f"x_loaded{s}") for s in range(2)]
        passed = sem("passed")
        ident_zero = sem("ident_zero")
        par_zero = sem("par_zero")
        top_i_ready = sem("top_i_ready")
        ident_ready = sem("ident_ready")
        bases_ready = sem("bases_ready")
        wT_psum = sem("wT_psum")
        wT_ready = sem("wT_ready")
        feat_turned = sem("feat_turned")
        featT_ready = sem("featT_ready")
        h_psum = sem("h_psum")
        h_ready = sem("h_ready")
        h_zeroed = sem("h_zeroed")
        adj_turned = sem("adj_turned")
        rem_turned = sem("rem_turned")
        piece_used = sem("piece_used")
        acc_done = sem("acc_done")
        g_ready = sem("g_ready")
        g_turned = sem("g_turned")
        ln_st = [sem(f"ln{n}_st") for n in (1, 2, 3)]
        ln_mv = [sem(f"ln{n}_mv") for n in (1, 2, 3)]
        ln_ve = [sem(f"ln{n}_ve") for n in (1, 2, 3)]
        ln_rs = [sem(f"ln{n}_rs") for n in (1, 2, 3)]
        xn1_ready = sem("xn1_ready")
        xn1_turned = sem("xn1_turned")
        xnT_ready = sem("xnT_ready")
        x1_ready = sem("x1_ready")
        w_all_ready = sem("w_all_ready")
        masks_ready = sem("masks_ready")
        mask_ready = sem("mask_ready")
        ranks_psum = sem("ranks_psum")
        pos_steps = sem("pos_steps")
        dest_ready = sem("dest_ready")
        place_next = sem("place_next")
        scattered = [sem(f"scattered{s}") for s in range(2)]
        table_steps = sem("table_steps")
        table_ready = sem("table_ready")
        filled = sem("filled")
        cols_ready = sem("cols_ready")
        xs_loaded = [sem(f"xs_loaded{s}") for s in range(2)]
        xs_turned = sem("xs_turned")
        xT_ready = sem("xT_ready")
        places_ready = sem("places_ready")
        w1_ready = sem("w1_ready")
        w2_ready = sem("w2_ready")
        up_psum = sem("up_psum")
        gelu_ready = sem("gelu_ready")
        y_psum = sem("y_psum")
        yT_ready = sem("yT_ready")
        y_turned = sem("y_turned")
        y_rows_ready = sem("y_rows_ready")
        place_now_ready = sem("place_now_ready")
        y_scattered = [sem(f"y_scattered{s}") for s in range(2)]
        picks_loaded = [sem(f"picks_loaded{s}") for s in range(2)]
        w_chunk_ready = sem("w_chunk_ready")
        first_added = sem("first_added")
        w1g_ready = sem("w1g_ready")
        fin_ready = sem("fin_ready")
        x1_stored = [sem(f"x1_stored{s}") for s in range(2)]
        xn2_ready = sem("xn2_ready")
        xn3_ready = sem("xn3_ready")
        xn2_turned = sem("xn2_turned")
        xn2T_ready = sem("xn2T_ready")
        logits_psum = sem("logits_psum")
        logits_ready = sem("logits_ready")
        top_ready = sem("top_ready")
        gap_ready = sem("gap_ready")
        egap_ready = sem("egap_ready")
        pick_steps = sem("pick_steps")
        w1_loaded = sem("w1_loaded")
        w2_loaded = sem("w2_loaded")
        par_turned = sem("par_turned")
        parT_ready = sem("parT_ready")
        b1_psum = sem("b1_psum")
        x1_loaded = [sem(f"x1_loaded{s}") for s in range(2)]
        out_stored = [sem(f"out_stored{s}") for s in range(2)]

        item_groups = [list(range(4 * q, min(4 * q + 4, KT))) for q in range(-(-KT // 4))]
        item_groups[-1].append(KT)
        NQ = len(item_groups)

        class At:

            def __init__(self, c, parity, before):
                self.c, self.s, self.before = c, parity, before
                self.fixed = isinstance(c, int)
                self.there = not self.fixed or 0 <= c <= LAST
                self.last = self.fixed and c == LAST

            def back(self, n):
                s = (self.s - n) % 2
                return At(self.c - n, s, self.before + (self.s - n - s) // 2)

            @property
            def n(self):
                return U_LAST if self.last else U

            def tiles(self):
                return [(t, t * P, min(P, self.n - t * P)) for t in range(-(-self.n // P))]

            def rows(self, a):
                return a[START_LAST:N, :] if self.last else self.span(a)

            def span(self, a):
                return a[self.c * U:self.c * U + U, :] if self.fixed else a[bass.ds(self.c * U, U), :]

            def own(self, a):
                return a[self.c, :, :] if self.fixed else a[bass.ds(self.c, 1), :, :].rearrange("a p n -> (a p) n")

        def chunks(eng, step, lo, lag, total=CH):
            hi = total - 2
            hi -= (hi - lo) % 2
            for c in range(lo):
                step(At(c, c % 2, c // 2))
            with eng.Fori(0, (hi - lo) // 2) as pair:
                for s in range(2):
                    step(At(pair * 2 + (lo + s), s, pair + lo // 2))
            for c in range(hi, total + lag):
                step(At(c, c % 2, c // 2))

        def after(eng, s, n):
            if not isinstance(n, int) or n > 0:
                eng.wait_ge(s, n)

        def wait_alone(eng, s, n):
            eng.wait_ge(s, n)
            eng.sem_inc(passed, 1)

        def load_adj(eng, k, i, ranges):
            after(eng, adj_turned, k.c * NP_ + (i - NAT + 1))
            rows = k.rows(adj)
            for g in ranges:
                eng.dma_start(nat[g * BLK:(g + 1) * BLK, i % NAT, 0:k.n // BLK, :],
                              rows[:, g * GI + i * J:g * GI + (i + 1) * J].rearrange("(r a) j -> a r j", a=BLK)
                              ).then_inc(nat_loaded[i % NAT], 16)

        def turn(pe, dst, src, k):
            for t, t0, m in k.tiles():
                ins = pe.transpose(dst[:, t0:t0 + m], src[0:m, t, :], ident[0:m, 0:m])
            return ins

        def turn_back(pe, dst, src, k):
            for t, t0, m in k.tiles():
                ins = pe.transpose(dst[0:m, t * D:(t + 1) * D], src[:, t0:t0 + m], ident[:])
            return ins

        def move_rows(eng, k, dst_of, src_of, whole, s, per_chunk):
            if not k.last:
                eng.dma_start(*whole).then_inc(s, 16)
            else:
                for t, t0, m in k.tiles():
                    eng.dma_start(dst_of(t, t0, m), src_of(t, t0, m)).then_inc(s, 16)

        LT = len(At(LAST, 0, 0).tiles())

        def moved(k):
            return (k.before + (LT if k.last else 1)) * 16

        def moved_picks(k):
            return (k.before + (LT if k.last else 1)) * (16 * K)

        def scatters(k):
            return (k.before * 4 + len(k.tiles())) * (K * 16)

        block = ctx.enter_context(nc.Block())

        @block.sync
        def _(sp):
            for g in range(NG):
                sp.dma_start(h_rows[g * BLK:(g + 1) * BLK, 0:KT, :],
                             item_feat[g * GI:(g + 1) * GI, :].rearrange("(k j) f -> j k f", j=BLK)
                             ).then_inc(feat_loaded, 16)
            sp.dma_start(h_rows[0:BLK, KT, :], item_feat[REM0:N, :]).then_inc(feat_loaded, 16)
            small = [(wi_nat, W_item), (wu_nat, W_user),
                     (bi_rows[:], b_item.rearrange("(a d) -> a d", a=1).broadcast_to([P, D])),
                     (br_rows[:], br.rearrange("(a d) -> a d", a=1).broadcast_to([P, E])),
                     (bu_col[:], b_user.rearrange("(d a) -> d a", a=1)), (wr_sb[:], Wr),
                     (par[0:E * HC, :], b1.rearrange("e (c p) -> (e c) p", p=P)),
                     (par[32:32 + E, :], ln_g), (par[64:64 + E, :], ln_b), (par[96:96 + E, :], b2)]
            assert len(small) == SMALL
            sp.wait_ge(par_zero, 1)
            for dst, src in small:
                sp.dma_start(dst, src).then_inc(consts_loaded, 16)

            def step(k):
                k2 = k.back(2)
                for i in range(NP_):
                    if k.there:
                        load_adj(sp, k, i, (0, 1))
                    if i == 1 and k.there:
                        after(sp, x1_ready, k.c - 1)
                        xr = k.rows(x)
                        move_rows(sp, k, lambda t, t0, m: xin[0:m, k.s, t, :], lambda t, t0, m: xr[t0:t0 + m, :],
                                  (xin[:, k.s, :, :], xr.rearrange("(t p) d -> p t d", p=P) if not k.last else None),
                                  x_loaded[k.s], 16)
                        after(sp, rem_turned, k.c)
                        sp.dma_start(rem_nat[:, 0:k.n // BLK, :],
                                     k.rows(adj)[:, REM0:N].rearrange("(r a) j -> a r j", a=BLK)
                                     ).then_inc(rem_loaded, 16)
                    if i == 2 and k2.there:
                        sp.wait_ge(x1_ready, k2.c + 1)
                        xr2 = k2.span(x1_dram)
                        move_rows(sp, k2, lambda t, t0, m: xr2[t0:t0 + m, :], lambda t, t0, m: x1[0:m, k2.s, t, :],
                                  (xr2.rearrange("(t p) d -> p t d", p=P), x1[:, k2.s, :, :]), x1_stored[k2.s], 16)

            chunks(sp, step, 6, 2)

            sp.wait_ge(adj_turned, CH * NP_)
            sp.dma_start(w1_sb, W1.rearrange("e d h -> d e h")).then_inc(w1_loaded, 16)
            for e in range(E):
                sp.dma_start(w2_sb[:, e, :, :], W2[e, :, :].rearrange("(c p) d -> p c d", p=P)).then_inc(w2_loaded, 16)
            for s in range(2):
                sp.wait_ge(x1_stored[s], moved(At(CH - 2 + s, s, CH // 2 - 1)))
                sp.wait_ge(scattered[s], scatters(At(CH - 2 + s, s, CH // 2 - 1)))
            sp.wait_ge(table_ready, 1)
            sp.wait_ge(masks_ready, 4)
            for e in range(E):
                end = sp.value_load(end_u[0:1, e:e + 1], min_val=e * CAP, max_val=(e + 1) * CAP - U)
                sp.dma_start(region_dram[bass.ds(end, U), :].rearrange("(t p) d -> p t d", p=P), fill).then_inc(filled, 16)
            sp.dma_start(region_dram[E * CAP:E * CAP + U, :].rearrange("(t p) d -> p t d", p=P), fill).then_inc(filled, 16)
            sp.wait_ge(filled, 16 * (E + 1))
            sp.wait_ge(acc_done, CH)

            def load_tile(k):
                if isinstance(k.c, int) and k.c >= NT:
                    return
                after(sp, xs_turned, k.c - 1)
                after(sp, places_ready, k.c - 1)
                start = sp.value_load(tab_row[0:1, k.c:k.c + 1] if k.fixed else tab_row[0:1, bass.ds(k.c, 1)],
                                      min_val=0, max_val=E * CAP)
                sp.dma_start(xs[:, k.s, :, :], region_dram[bass.ds(start, U), :].rearrange("(t p) d -> p t d", p=P)
                             ).then_inc(xs_loaded[k.s], 16)

            chunks(sp, load_tile, 2, 0, NT)

            for s in range(2):
                sp.wait_ge(y_scattered[s], NT // 2 * 64)

            def combine(k):
                if k.there:
                    after(sp, fin_ready, k.c - 1)
                    for n in range(K):
                        at = picks_dram[n * PLACES:(n + 1) * PLACES, :]
                        pr = k.span(at)
                        move_rows(sp, k, lambda t, t0, m: picks[0:m, k.s, n, t, :], lambda t, t0, m: pr[t0:t0 + m, :],
                                  (picks[:, k.s, n, :, :], pr.rearrange("(t p) d -> p t d", p=P)), picks_loaded[k.s], 16)
                    xr = k.span(x1_dram)
                    move_rows(sp, k, lambda t, t0, m: x1[0:m, k.s, t, :], lambda t, t0, m: xr[t0:t0 + m, :],
                              (x1[:, k.s, :, :], xr.rearrange("(t p) d -> p t d", p=P)), x1_loaded[k.s], 16)
                b = k.back(2)
                if b.there:
                    sp.wait_ge(fin_ready, b.c + 1)
                    o = b.rows(out)
                    skip = LAST * U - START_LAST
                    move_rows(sp, b, lambda t, t0, m: o[t0 + (skip if t == 0 else 0):t0 + m, :],
                              lambda t, t0, m: fin[(skip if t == 0 else 0):m, b.s, t, :],
                              (o.rearrange("(t p) d -> p t d", p=P) if not b.last else None, fin[:, b.s, :, :]),
                              out_stored[b.s], 16)

            chunks(sp, combine, 4, 2)
            for s in range(2):
                sp.wait_ge(out_stored[s], moved(At(CH - 2 + s, s, CH // 2 - 1)))

        @block.scalar
        def _(act):
            for i in range(NAT):
                load_adj(act, At(0, 0, 0), i, (2, 3))
            act.wait_ge(wT_psum, 2)
            act.activation(wiT[:], ps_x[:, 0:D], ACT.Copy).then_inc(wT_ready, 1)
            act.activation(wuT[:], ps_x[:, D:2 * D], ACT.Copy).then_inc(wT_ready, 1)
            act.wait_ge(par_turned, 1)
            act.activation(parT[:], ps_g[:, 0:P], ACT.Copy).then_inc(parT_ready, 1)
            for q in range(NQ):
                act.wait_ge(feat_turned, q + 1)
                after(act, h_psum, q - 1)
                w = P * len(item_groups[q]) - (P - BLK) * (q == NQ - 1)
                act.activation(featT[:, q % 2, 0:w], bank[4 + q % 2][:, 0:w], ACT.Copy).then_inc(featT_ready, 1)

            def step(k):
                k1, k2 = k.back(1), k.back(2)
                for i in range(NP_):
                    if k.there and not (k.fixed and k.c == 0 and i < NAT):
                        load_adj(act, k, i, (2, 3))
                    if i == 4 and k1.there:
                        act.wait_ge(acc_done, k1.c + 1)
                        after(act, g_turned, k1.c)
                        act.activation(gT[:, 0:k1.n], acc[k1.s][:, 0:k1.n], ACT.Relu,
                                       bias=bu_col[:, 0:1]).then_inc(g_ready, 1)
                    if i == 5 and k.there:
                        act.wait_ge(xn1_turned, k.c + 1)
                        after(act, acc_done, k.c)
                        act.activation(xnT[:, 0:k.n], ps_x[:, 0:k.n], ACT.Copy).then_inc(xnT_ready, 1)
                    if i == 5 and k2.there:
                        act.wait_ge(xn2_turned, k2.c + 1)
                        after(act, logits_psum, k2.c)
                        act.activation(xn2T[:, 0:k2.n], ps_n2[:, 0:k2.n], ACT.Copy).then_inc(xn2T_ready, 1)

            chunks(act, step, 6, 2)

            def tile(k):
                b = k.back(2)
                if not k.fixed or k.c < NT:
                    after(act, y_psum, k.c - 1)
                    act.wait_ge(w1_ready, k.c + 1)
                    for m in range(HC):
                        act.wait_ge(up_psum, k.c * HC + (m + 1))
                        act.activation(hT[:, k.s, m, :], bank[m][:], ACT.Gelu, bias=b1s[:, k.s, m:m + 1]
                                       ).then_inc(gelu_ready, 1)
                if not k.fixed or k.c >= 2:
                    act.wait_ge(y_turned, b.c + 1)
                    after(act, y_scattered[b.s], b.before * 64)
                    act.activation(y_rows[:, b.s, :, :].rearrange("p t d -> p (t d)"), ps_l[:], ACT.Copy
                                   ).then_inc(y_rows_ready, 1)

            chunks(act, tile, 4, 2, NT)

        @block.gpsimd
        def _(pool):
            pool.memset(ident[:], 0.0).then_inc(ident_zero, 1)
            pool.wait_ge(ident_zero, 1)
            pool.affine_select(out=ident[:], in_=ident[:], compare_op=ALU.not_equal, fill=1.0, base=0,
                               pattern=[[-1, P]], channel_multiplier=1).then_inc(ident_ready, 1)
            pool.memset(par, 0.0).then_inc(par_zero, 1)
            pool.iota(iota_e[:], [[1, E]], base=0, channel_multiplier=0,
                      allow_small_or_imprecise_dtypes=True).then_inc(bases_ready, 1)
            pool.memset(half_neg[:], -0.5).then_inc(bases_ready, 1)
            pool.memset(base_e[:], E_CONST).then_inc(bases_ready, 1)
            pool.memset(eps4[:], EPS).then_inc(bases_ready, 1)
            pool.memset(ones[:], 1.0).then_inc(masks_ready, 1)
            pool.wait_ge(masks_ready, 1)
            pool.affine_select(out=before_me[:], in_=ones[:], compare_op=ALU.is_gt, fill=0.0, base=0,
                               pattern=[[1, P]], channel_multiplier=-1).then_inc(masks_ready, 1)
            big = dict(channel_multiplier=0, allow_small_or_imprecise_dtypes=True)
            pool.iota(region_end[:], [[CAP, E]], base=0, **big).then_inc(bases_ready, 1)
            pool.iota(place_f[:], [[PLACES, K], [P, 4]], base=0, channel_multiplier=1,
                      allow_small_or_imprecise_dtypes=True).then_inc(bases_ready, 1)
            pool.iota(steps_512[:], [[U, CH + 1]], base=0, **big).then_inc(bases_ready, 1)
            pool.iota(upto[:], [[1, E], [-1, E]], base=0, **big).then_inc(bases_ready, 1)
            pool.iota(tile_no[:], [[1, NT]], base=0, **big).then_inc(bases_ready, 1)
            pool.wait_ge(bases_ready, 9)

            def rstd(n, k):
                T = len(k.tiles())
                pool.wait_ge(ln_mv[n], k.c + 1)
                pool.tensor_tensor(ve[n][:, 0:T], mv[n][:, 0:T, 1], eps4[:, 0:T], ALU.add).then_inc(ln_ve[n], 1)
                pool.wait_ge(ln_ve[n], k.c + 1)
                pool.tensor_tensor(rs[n][:, 0:T], ve[n][:, 0:T], half_neg[:, 0:T], ALU.pow).then_inc(ln_rs[n], 1)

            def step(k):
                k1, k2, k3 = k.back(1), k.back(2), k.back(3)
                if k.there:
                    rstd(0, k)
                if k3.there:
                    wait_alone(pool, dest_ready, k3.c + 1)
                    for t, t0, m in k3.tiles():
                        for n in range(K):
                            pool.indirect_dma_start(
                                out=region_dram, out_offset=bass.IndirectOffsetOnAxis(
                                    ap=dest[0:m, k3.s, n * 4 + t:n * 4 + t + 1], axis=0),
                                in_=rows[0:m, k3.s, t, n, :], in_offset=None).then_inc(scattered[k3.s], 16)
                if k1.there:
                    rstd(1, k1)
                    rstd(2, k1)
                if k2.there:
                    T = len(k2.tiles())
                    pool.wait_ge(gap_ready, k2.c + 1)
                    pool.tensor_tensor(egap[:, 0:T], base_e[:, 0:T], gap[:, 0:T], ALU.pow).then_inc(egap_ready, 1)

            chunks(pool, step, 6, 3)
            pool.wait_ge(scattered[0], scatters(At(CH - 2, 0, CH // 2 - 1)))
            pool.memset(fill, 0.0).then_inc(masks_ready, 1)
            pool.wait_ge(masks_ready, 3)
            pool.iota(fill[:, :, D].bitcast(U32), [[0, 4]], base=NOWHERE, channel_multiplier=0).then_inc(masks_ready, 1)

            def tile(k):
                wait_alone(pool, places_ready, k.c + 1)
                if not k.fixed or k.c >= 2:
                    wait_alone(pool, y_scattered[k.s], k.before * 64)
                pool.tensor_copy(place_now[:, k.s, :], places[:, bass.ds(k.c * 4, 4)] if not k.fixed
                                 else places[:, k.c * 4:k.c * 4 + 4]).then_inc(place_now_ready, 1)
                wait_alone(pool, place_now_ready, k.c + 1)
                wait_alone(pool, y_rows_ready, k.c + 1)
                for t in range(4):
                    pool.indirect_dma_start(
                        out=picks_dram, out_offset=bass.IndirectOffsetOnAxis(ap=place_now[:, k.s, t:t + 1], axis=0),
                        in_=y_rows[:, k.s, t, :], in_offset=None, bounds_check=K * PLACES - 1, oob_is_err=False
                        ).then_inc(y_scattered[k.s], 16)

            chunks(pool, tile, 2, 0, NT)

        @block.tensor
        def _(pe):
            pe.wait_ge(ident_ready, 1)
            pe.wait_ge(consts_loaded, 16 * SMALL)
            pe.transpose(ps_x[:, 0:D], wi_nat, ident[:]).then_inc(wT_psum, 1)
            pe.transpose(ps_x[:, D:2 * D], wu_nat, ident[:]).then_inc(wT_psum, 1)
            pe.transpose(ps_g[:, 0:P], par, ident[:]).then_inc(par_turned, 1)

            pe.wait_ge(feat_loaded, 16 * (NG + 1))
            pe.wait_ge(wT_ready, 2)
            for q in range(NQ + 1):
                if q < NQ:
                    after(pe, featT_ready, q - 1)
                    for n, t in enumerate(item_groups[q]):
                        m = BLK if t == KT else P
                        ins = pe.transpose(bank[4 + q % 2][:, n * P:n * P + m], h_rows[0:m, t, :], ident[0:m, 0:m])
                    ins.then_inc(feat_turned, 1)
                if q > 0:
                    b = q - 1
                    pe.wait_ge(featT_ready, b + 1)
                    after(pe, h_ready, b - 1)
                    for n, t in enumerate(item_groups[b]):
                        m = BLK if t == KT else P
                        ins = pe.matmul(bank[6 + b % 2][0:m, n * P:(n + 1) * P], featT[:, b % 2, n * P:n * P + m],
                                        wiT[:], start=True, stop=True)
                    ins.then_inc(h_psum, 1)
            pe.wait_ge(h_zeroed, 1)

            def step(k):
                k1, k2 = k.back(1), k.back(2)
                for i in range(NP_):
                    if k.there:
                        if i == 0:
                            after(pe, g_ready, k.c - 1)
                        pe.wait_ge(adj_turned, k.c * NP_ + (i + 1))
                        for j in range(KP):
                            ins = pe.matmul(acc[k.s][:, 0:k.n], h_rows[:, i * KP + j, :], adjT[:, i % TS, j, 0:k.n],
                                            start=(i == 0 and j == 0), stop=False)
                        ins.then_inc(piece_used, 1)
                    if i == 0 and k.there:
                        pe.wait_ge(xn1_ready, k.c + 1)
                        after(pe, xnT_ready, k.c)
                        turn(pe, ps_x, xn1, k).then_inc(xn1_turned, 1)
                    if i == 1 and k1.there:
                        pe.wait_ge(g_ready, k1.c + 1)
                        after(pe, x1_ready, k1.c)
                        turn_back(pe, ps_g, gT, k1).then_inc(g_turned, 1)
                    if i == 2 and k2.there:
                        pe.wait_ge(xn2T_ready, k2.c + 1)
                        after(pe, logits_ready, k2.c)
                        for t, t0, m in k2.tiles():
                            ins = pe.matmul(ps_l[0:m, t * E:(t + 1) * E], xn2T[:, t0:t0 + m], wr_sb[:],
                                            start=True, stop=True)
                        ins.then_inc(logits_psum, 1)
                    if i == 4 and k.there:
                        pe.wait_ge(xnT_ready, k.c + 1)
                        pe.matmul(acc[k.s][:, 0:k.n], wuT[:], xnT[:, 0:k.n], start=False, stop=False)
                    if i == 5 and k1.there:
                        pe.wait_ge(xn2_ready, k1.c + 1)
                        after(pe, xn2T_ready, k1.c)
                        turn(pe, ps_n2, xn2, k1).then_inc(xn2_turned, 1)
                    if i == 5 and k2.there:
                        pe.wait_ge(mask_ready, k2.c + 1)
                        after(pe, dest_ready, k2.c)
                        for t, t0, m in k2.tiles():
                            pe.matmul(ps_w[:, t * E:(t + 1) * E], before_me[0:m, :], mask[0:m, t, :],
                                      start=True, stop=(t == 0))
                            for b in range(t):
                                pe.matmul(ps_w[:, t * E:(t + 1) * E], ones[:], mask[:, b, :],
                                          start=False, stop=(b == t - 1))
                        for t, t0, m in k2.tiles():
                            ins = pe.matmul(ps_w[:, 4 * E:5 * E], ones[0:m, :], mask[0:m, t, :],
                                            start=(t == 0), stop=(m < P or t == 3))
                        ins.then_inc(ranks_psum, 1)
                if k.there:
                    pe.wait_ge(rem_turned, k.c + 1)
                    pe.matmul(acc[k.s][:, 0:k.n], h_rows[0:BLK, KT, :], rem_T[:, 0:k.n],
                              start=False, stop=True).then_inc(acc_done, 1)

            chunks(pe, step, 6, 2)

            pe.wait_ge(w1_loaded, 16)
            pe.wait_ge(dest_ready, CH)
            for e in range(E):
                for m in range(HC):
                    ins = pe.matmul(ps_w[:, e * HC + m:e * HC + m + 1], w1_sb[:, e, m * P:(m + 1) * P],
                                    parT[:, 64 + e:65 + e], start=True, stop=True)
            ins.then_inc(b1_psum, 1)
            pe.wait_ge(w1g_ready, E)
            pe.wait_ge(g_ready, CH)
            pe.wait_ge(x1_ready, CH)
            pe.wait_ge(xn2T_ready, CH)
            pe.wait_ge(logits_ready, CH)
            whole = At(0, 0, 0)

            def turn_in(k):
                pe.wait_ge(xs_loaded[k.s], (k.before + 1) * 16)
                after(pe, xT_ready, k.c)
                turn(pe, bank[4], xs[:, k.s, :, 0:D], whole).then_inc(xs_turned, 1)

            def tile(k):
                b, bb, nxt = k.back(1), k.back(2), k.back(-1)
                if k.fixed and k.c == 0:
                    turn_in(k)
                if not k.fixed or k.c < NT:
                    pe.wait_ge(xT_ready, k.c + 1)
                    pe.wait_ge(w1_ready, k.c + 1)
                    for m in range(HC):
                        after(pe, gelu_ready, k.c * HC + (m + 1 - HC))
                        pe.matmul(bank[m][:], w1s[:, k.s, m * P:(m + 1) * P], xT[:, k.s, :],
                                  start=True, stop=True).then_inc(up_psum, 1)
                if not k.fixed or nxt.c < NT:
                    turn_in(nxt)
                if not k.fixed or 0 <= b.c < NT:
                    pe.wait_ge(w2_ready, b.c + 1)
                    after(pe, yT_ready, b.c)
                    for m in range(HC):
                        pe.wait_ge(gelu_ready, b.c * HC + (m + 1))
                        ins = pe.matmul(bank[5][:], w2s[:, b.s, m, :], hT[:, b.s, m, :],
                                        start=(m == 0), stop=(m == HC - 1))
                    ins.then_inc(y_psum, 1)
                if not k.fixed or 0 <= bb.c < NT:
                    pe.wait_ge(yT_ready, bb.c + 1)
                    after(pe, y_rows_ready, bb.c)
                    turn_back(pe, ps_l, yT, whole).then_inc(y_turned, 1)

            chunks(pe, tile, 4, 2, NT)

        @block.vector
        def _(dve):
            dve.wait_ge(consts_loaded, 16 * SMALL)
            for q in range(NQ):
                dve.wait_ge(h_psum, q + 1)
                for n, t in enumerate(item_groups[q]):
                    if t == KT:
                        dve.tensor_tensor(h_rows[0:BLK, t, :], bank[6 + q % 2][0:BLK, n * P:(n + 1) * P],
                                          bi_rows[0:BLK, :], ALU.add).then_inc(h_ready, 1)
                full = [t for t in item_groups[q] if t < KT]
                w = len(full)
                ins = dve.tensor_tensor(h_rows[:, full[0]:full[0] + w, :],
                                        bank[6 + q % 2][:, 0:w * P].rearrange("p (k d) -> p k d", d=D),
                                        bi_rows[:].unsqueeze(1).to_broadcast([P, w, D]), ALU.add)
                ins.then_inc(h_ready, 1)
            dve.wait_ge(h_ready, NQ + 1)
            dve.memset(h_rows[0:REM_OLD, KT, :], 0.0).then_inc(h_zeroed, 1)

            def stats(n, src, k):
                after(dve, ln_rs[n], k.c)
                for t, t0, m in k.tiles():
                    ins = dve.bn_stats(st[n][0:m, t, :], src[0:m, t, :])
                ins.then_inc(ln_st[n], 1)

            def aggregate(n, k):
                wait_alone(dve, ln_st[n], k.c + 1)
                for t, t0, m in k.tiles():
                    ins = dve.bn_aggr(mv[n][0:m, t, :], st[n][0:m, t, :])
                ins.then_inc(ln_mv[n], 1)

            def normalise(n, dst, src, k, done):
                dve.wait_ge(ln_rs[n], k.c + 1)
                for t, t0, m in k.tiles():
                    ins = dve.tensor_scalar(dst[0:m, t, :], src[0:m, t, :], mv[n][0:m, t, 0:1], rs[n][0:m, t:t + 1],
                                            ALU.subtract, ALU.mult)
                ins.then_inc(done, 1)

            def step(k):
                k1, k2, k3 = k.back(1), k.back(2), k.back(3)
                for i in range(NP_):
                    if k.there:
                        dve.wait_ge(nat_loaded[i % NAT], (k.c * (NP_ // NAT) + (i // NAT + 1)) * (16 * NG))
                        after(dve, piece_used, k.c * NP_ + (i - TS + 1))
                        r = k.n // BLK
                        dve.transpose(adjT[:, i % TS, :, 0:k.n].rearrange("p k (r a) -> p r k a", a=BLK),
                                      nat[:, i % NAT, 0:r, :].rearrange("p r (k j) -> p r k j", j=BLK)
                                      ).then_inc(adj_turned, 1)
                    if i == 0 and k.there:
                        xk = xin[:, k.s, :, :]
                        dve.wait_ge(x_loaded[k.s], moved(k))
                        stats(0, xk, k)
                        aggregate(0, k)
                    if i == 1 and k.there:
                        after(dve, xn1_turned, k.c)
                        normalise(0, xn1, xin[:, k.s, :, :], k, xn1_ready)
                    if i == 3 and k.there:
                        dve.wait_ge(rem_loaded, k.c * 16 + 16)
                        after(dve, acc_done, k.c)
                        dve.transpose(rem_T[:, 0:k.n], rem_nat[:, 0:k.n // BLK, :].rearrange("p r j -> p (r j)")
                                      ).then_inc(rem_turned, 1)
                    if i == 3 and k1.there:
                        dve.wait_ge(g_turned, k1.c + 1)
                        after(dve, x1_stored[k1.s], k1.before * 16)
                        for t, t0, m in k1.tiles():
                            ins = dve.tensor_tensor(x1[0:m, k1.s, t, :], ps_g[0:m, t * D:(t + 1) * D],
                                                    xin[0:m, k1.s, t, :], ALU.add)
                        ins.then_inc(x1_ready, 1)
                        dve.wait_ge(x1_ready, k1.c + 1)
                        stats(1, x1[:, k1.s, :, :], k1)
                        aggregate(1, k1)
                    if i == 1 and k3.there:
                        destinations(k3)
                    if i == 4 and k1.there:
                        after(dve, xn2_turned, k1.c)
                        normalise(1, xn2, x1[:, k1.s, :, :], k1, xn2_ready)
                        dve.wait_ge(xn2_ready, k1.c + 1)
                        stats(2, xn2, k1)
                        aggregate(2, k1)
                    if i == 4 and k2.there:
                        route_top(k2)
                    if i == 5 and k1.there:
                        after(dve, scattered[k1.s], k1.before * (4 * K * 16))
                        dve.wait_ge(ln_rs[2], k1.c + 1)
                        for t, t0, m in k1.tiles():
                            for n in range(K):
                                dve.tensor_scalar(rows[0:m, k1.s, t, n, 0:D], xn2[0:m, t, :], mv[2][0:m, t, 0:1],
                                                  rs[2][0:m, t:t + 1], ALU.subtract, ALU.mult)
                        after(dve, place_next, k1.c)
                        T = len(k1.tiles())
                        for n in range(K):
                            ins = dve.tensor_copy(rows[:, k1.s, 0:T, n, D].bitcast(U32), place_f[:, n, 0:T])
                        ins.then_inc(xn3_ready, 1)
                        dve.wait_ge(xn3_ready, k1.c + 1)
                        dve.tensor_scalar(place_f[:], place_f[:], float(U), None, ALU.add).then_inc(place_next, 1)
                    if i == 5 and k2.there:
                        route_weights(k2)

            def route_top(k):
                T, c = len(k.tiles()), k.c
                dve.wait_ge(logits_psum, c + 1)
                for t, t0, m in k.tiles():
                    ins = dve.tensor_tensor(logit[0:m, t, :], ps_l[0:m, t * E:(t + 1) * E], br_rows[0:m, :], ALU.add)
                ins.then_inc(logits_ready, 1)
                wait_alone(dve, logits_ready, c + 1)
                for t, t0, m in k.tiles():
                    ins = dve.max(top[0:m, t, :], logit[0:m, t, :])
                ins.then_inc(top_ready, 1)
                wait_alone(dve, top_ready, c + 1)
                for t, t0, m in k.tiles():
                    ins = dve.max_index(top_i[0:m, t, :], top[0:m, t, :], logit[0:m, t, :])
                ins.then_inc(top_i_ready, 1)
                dve.wait_ge(top_i_ready, c + 1)
                dve.tensor_copy(top_f[:, 0:T, :], top_i[:, 0:T, 0:2])
                dve.tensor_tensor(gap[:, 0:T], top[:, 0:T, 1], top[:, 0:T, 0], ALU.subtract).then_inc(gap_ready, 1)

            def route_weights(k):
                T, c = len(k.tiles()), k.c
                dve.wait_ge(egap_ready, c + 1)
                dve.tensor_scalar(esum[:, 0:T], egap[:, 0:T], 1.0, None, ALU.add).then_inc(pick_steps, 1)
                after(dve, pos_steps, c * 4)
                for n in range(K):
                    for t in range(T):
                        ins = dve.tensor_scalar(is_pick[:, n, t, :], iota_e[:], top_f[:, t, n:n + 1], None, ALU.is_equal)
                ins.then_inc(pick_steps, 1)
                dve.wait_ge(pick_steps, c * 4 + 2)
                after(dve, w_all_ready, c)
                dve.reciprocal(pick_w[:, 0:T, 0], esum[:, 0:T]).then_inc(pick_steps, 1)
                after(dve, ranks_psum, c)
                dve.tensor_tensor(mask[:, 0:T, :], is_pick[:, 0, 0:T, :], is_pick[:, 1, 0:T, :], ALU.add
                                  ).then_inc(mask_ready, 1)
                dve.wait_ge(pick_steps, c * 4 + 3)
                dve.tensor_tensor(pick_w[:, 0:T, 1], egap[:, 0:T], pick_w[:, 0:T, 0], ALU.mult).then_inc(pick_steps, 1)
                wait_alone(dve, pick_steps, c * 4 + 4)
                n = T * K
                dve.tensor_copy(w_all[:, c * 8:c * 8 + n] if k.fixed else w_all[:, bass.ds(c * 8, n)],
                                pick_w[:, 0:T, :].rearrange("p t n -> p (t n)")).then_inc(w_all_ready, 1)

            def destinations(k):
                T, c = len(k.tiles()), k.c
                dve.wait_ge(ranks_psum, c + 1)
                after(dve, pos_steps, c * 4)
                dve.tensor_tensor(pos[:, 0:T, :], ps_w[:, 0:T * E].rearrange("p (t e) -> p t e", e=E),
                                  region_end[:].unsqueeze(1).to_broadcast([P, T, E]), ALU.add).then_inc(pos_steps, 1)
                dve.wait_ge(pos_steps, c * 4 + 1)
                dve.tensor_tensor(region_end[:], ps_w[:, 4 * E:5 * E], region_end[:], ALU.add).then_inc(pos_steps, 1)
                for n in range(K):
                    ins = dve.tensor_tensor(pos_pick[:, n, 0:T, :], is_pick[:, n, 0:T, :], pos[:, 0:T, :], ALU.mult)
                ins.then_inc(pos_steps, 1)
                dve.wait_ge(pos_steps, c * 4 + 3)
                for n in range(K):
                    ins = dve.tensor_reduce(dest_f[:, n, 0:T], pos_pick[:, n, 0:T, :], AX.X, ALU.add)
                ins.then_inc(pos_steps, 1)
                dve.wait_ge(pos_steps, c * 4 + 4)
                after(dve, scattered[k.s], k.before * (4 * K * 16))
                for n in range(K):
                    ins = dve.tensor_copy(dest[:, k.s, n * 4:n * 4 + T], dest_f[:, n, 0:T])
                ins.then_inc(dest_ready, 1)

            chunks(dve, step, 6, 3)

            made = [0]

            def table(ins):
                made[0] += 1
                ins.then_inc(table_steps, 1)
                dve.wait_ge(table_steps, made[0])

            dve.wait_ge(pos_steps, CH * 4)
            dve.tensor_copy(end_u[:], region_end[0:1, :])
            table(dve.tensor_scalar(count[:], iota_e[0:1, :], -float(CAP), None, ALU.mult))
            table(dve.tensor_tensor(count[:], region_end[0:1, :], count[:], ALU.add))
            table(dve.tensor_tensor(over, count[:].unsqueeze(2).to_broadcast([1, E, CH + 1]),
                                    steps_512[:].unsqueeze(1).to_broadcast([1, E, CH + 1]), ALU.is_gt))
            table(dve.tensor_reduce(n_tiles[:], over, AX.X, ALU.add))
            table(dve.tensor_scalar(upto[:], upto[:], 0.0, None, ALU.is_ge))
            table(dve.tensor_tensor(upto_n[:], upto[:], n_tiles[:].unsqueeze(1).to_broadcast([1, E, E]), ALU.mult))
            table(dve.tensor_reduce(last_tile[:], upto_n[:], AX.X, ALU.add))
            table(dve.tensor_tensor(past, tile_no[:].unsqueeze(2).to_broadcast([1, NT, E]),
                                    last_tile[:].unsqueeze(1).to_broadcast([1, NT, E]), ALU.is_ge))
            table(dve.tensor_tensor(past_n, past, n_tiles[:].unsqueeze(1).to_broadcast([1, NT, E]), ALU.mult))
            table(dve.tensor_reduce(tab_past[:], past, AX.X, ALU.add))
            table(dve.tensor_reduce(tab_n[:], past_n, AX.X, ALU.add))
            table(dve.tensor_tensor(tab_rel[:], tile_no[:], tab_n[:], ALU.subtract))
            table(dve.tensor_scalar(tab_rel[:], tab_rel[:], float(U), None, ALU.mult))
            table(dve.scalar_tensor_tensor(out=tab_rowf[:], in0=tab_past[:], scalar=float(CAP), in1=tab_rel[:],
                                           op0=ALU.mult, op1=ALU.add))
            table(dve.tensor_scalar(tab_rowf[:], tab_rowf[:], float(E * CAP), None, ALU.min))
            table(dve.tensor_scalar(tab_past[:], tab_past[:], float(E - 1), None, ALU.min))
            dve.tensor_copy(tab_row[:], tab_rowf[:])
            table(dve.tensor_copy(tab_e[:], tab_past[:]))
            dve.wait_ge(ident_ready, 1)
            dve.memset(count[:], 0.0).then_inc(table_ready, 1)

            dve.wait_ge(parT_ready, 1)
            dve.wait_ge(b1_psum, 1)
            dve.tensor_tensor(cols[:, :, 0:HC], ps_w[:, 0:E * HC].rearrange("p (e c) -> p e c", e=E),
                              parT[:, 0:E * HC].rearrange("p (e c) -> p e c", e=E), ALU.add)
            dve.tensor_copy(cols[:, :, HC], parT[:, 96:96 + E]).then_inc(cols_ready, 1)
            for e in range(E):
                dve.tensor_scalar(w1_sb[:, e, :], w1_sb[:, e, :], parT[:, 32 + e:33 + e], None, ALU.mult
                                  ).then_inc(w1g_ready, 1)
            dve.wait_ge(cols_ready, 1)
            dve.wait_ge(w1g_ready, E)
            dve.wait_ge(w2_loaded, 16 * E)

            def expert_of(k):
                return dve.value_load(tab_e[0:1, k.c:k.c + 1] if k.fixed else tab_e[0:1, bass.ds(k.c, 1)],
                                      min_val=0, max_val=E - 1)

            def first_weights(k):
                if k.fixed and k.c >= NT:
                    return
                e = expert_of(k)
                if not k.fixed or k.c >= 2:
                    wait_alone(dve, up_psum, (k.c - 1) * HC)
                    wait_alone(dve, gelu_ready, (k.c - 1) * HC)
                w1f = w1_sb.rearrange("p e h -> p (e h)")
                cf = cols.rearrange("p e c -> p (e c)")
                dve.tensor_copy(w1s[:, k.s, :], w1f[:, bass.ds(e * H, H)])
                dve.tensor_copy(b1s[:, k.s, :], cf[:, bass.ds(e * (HC + 1), HC)]).then_inc(w1_ready, 1)

            def second_weights(k):
                if k.fixed and k.c >= NT:
                    return
                e = expert_of(k)
                if not k.fixed or k.c >= 2:
                    wait_alone(dve, yT_ready, k.c - 1)
                w2f = w2_sb.rearrange("p e c d -> p (e c d)")
                cf = cols.rearrange("p e c -> p (e c)")
                dve.tensor_copy(b2s[:, k.s, :], cf[:, bass.ds(e * (HC + 1) + HC, 1)])
                dve.tensor_copy(w2s[:, k.s, :, :].rearrange("p c d -> p (c d)"), w2f[:, bass.ds(e * H, H)]
                                ).then_inc(w2_ready, 1)

            def rows_in(k):
                if k.fixed and k.c >= NT:
                    return
                dve.wait_ge(xs_turned, k.c + 1)
                after(dve, up_psum, (k.c - 1) * HC)
                dve.tensor_copy(xT[:, k.s, :], bank[4][:]).then_inc(xT_ready, 1)
                wait_alone(dve, xs_loaded[k.s], (k.before + 1) * 16)
                dve.tensor_copy(places[:, bass.ds(k.c * 4, 4)] if not k.fixed else places[:, k.c * 4:k.c * 4 + 4],
                                xs[:, k.s, :, D].bitcast(U32)).then_inc(places_ready, 1)

            for c in range(2):
                first_weights(At(c, c, 0))
            second_weights(At(0, 0, 0))
            rows_in(At(0, 0, 0))

            def tile(k):
                b, nxt = k.back(1), k.back(-1)
                rows_in(nxt)
                if not k.fixed or 0 <= b.c < NT:
                    dve.wait_ge(y_psum, b.c + 1)
                    after(dve, y_turned, b.c)
                    dve.tensor_scalar(yT, bank[5][:], b2s[:, b.s, :], None, ALU.add).then_inc(yT_ready, 1)
                second_weights(nxt)
                first_weights(nxt.back(-1))

            chunks(dve, tile, 4, 1, NT)

            def combine(k):
                T, n = len(k.tiles()), len(k.tiles()) * K
                dve.tensor_copy(w_chunk[:, k.s, 0:n], w_all[:, bass.ds(k.c * 8, n)] if not k.fixed
                                else w_all[:, k.c * 8:k.c * 8 + n]).then_inc(w_chunk_ready, 1)
                dve.wait_ge(w_chunk_ready, k.c + 1)
                dve.wait_ge(x1_loaded[k.s], moved(k))
                dve.wait_ge(picks_loaded[k.s], moved_picks(k))
                for t, t0, m in k.tiles():
                    ins = dve.scalar_tensor_tensor(out=x1[0:m, k.s, t, :], in0=picks[0:m, k.s, 0, t, :],
                                                   scalar=w_chunk[0:m, k.s, K * t:K * t + 1], in1=x1[0:m, k.s, t, :],
                                                   op0=ALU.mult, op1=ALU.add)
                ins.then_inc(first_added, 1)
                dve.wait_ge(first_added, k.c + 1)
                after(dve, out_stored[k.s], k.before * 16)
                for t, t0, m in k.tiles():
                    ins = dve.scalar_tensor_tensor(out=fin[0:m, k.s, t, :], in0=picks[0:m, k.s, 1, t, :],
                                                   scalar=w_chunk[0:m, k.s, K * t + 1:K * t + 2],
                                                   in1=x1[0:m, k.s, t, :], op0=ALU.mult, op1=ALU.add)
                ins.then_inc(fin_ready, 1)

            chunks(dve, combine, 2, 0)


_INS = ['x', 'adj', 'L0_gnn_item_feat', 'L0_gnn_W_item', 'L0_gnn_b_item', 'L0_gnn_W_user', 'L0_gnn_b_user',
        'L0_ffn_Wr', 'L0_ffn_br', 'L0_ffn_ln_g', 'L0_ffn_ln_b', 'L0_ffn_W1', 'L0_ffn_b1', 'L0_ffn_W2', 'L0_ffn_b2']


def kernel(**inputs):
    import numpy as np
    from concourse import bacc
    from concourse.bass_utils import run_bass_kernel_spmd

    nc = bacc.Bacc("TRN2", target_bir_lowering=False, num_devices=1)
    arrays, args = {}, []
    for name in _INS:
        a = np.ascontiguousarray(inputs[name])
        arrays["in_" + name] = a
        args.append(nc.dram_tensor("in_" + name, a.shape, mybir.dt.from_np(a.dtype), kind="ExternalInput").ap())
    res = nc.dram_tensor("out_rows", list(arrays["in_x"].shape), F32, kind="ExternalOutput").ap()
    graph_moe_kernel(nc, *args, res)
    r = run_bass_kernel_spmd(nc, [arrays], core_ids=[0])
    return r.results[0]["out_rows"]
```

```python
from contextlib import ExitStack

import concourse.bass as bass
from concourse import mybir

F32 = mybir.dt.float32
F32R = mybir.dt.float32r
U32 = mybir.dt.uint32
BF16 = mybir.dt.bfloat16
AX = mybir.AxisListType
ALU = mybir.AluOpType
ACT = mybir.ActivationFunctionType

P = 128
BLK = 32
EPS = 1e-5
E_CONST = 2.718281828459045


def graph_moe_kernel(nc, x, adj, item_feat, W_item, b_item, W_user, b_user,
                     Wr, br, ln_g, ln_b, W1, b1, W2, b2, out):
    N, D = x.shape
    E, _, H = W1.shape
    HC = H // P
    NG = P // BLK
    KT = N // P
    GI = KT * BLK
    REM0 = N - BLK
    REM_OLD = BLK - (N - KT * P)
    PIECES = 6
    KP = KT // PIECES
    J = KP * BLK
    U = 512
    R = U // BLK
    CH = -(-N // U)
    LAST = CH - 1
    U_LAST = -(-(N - LAST * U) // BLK) * BLK
    START_LAST = N - U_LAST
    NAT = 4
    HR = R // 2
    SPLIT = 5
    WHOLE = KP - SPLIT
    TS = 2
    SMALL = 7
    FEAT_PARTS = [(0, 8), (8, 32), (32, KT)]
    assert D == P and GI * NG == KT * P and KP * PIECES == KT and 2 * PIECES % NAT == 0 and PIECES % TS == 0

    K = 2
    ROW = D + 2
    SLOTS = (LAST * U + U_LAST) * K
    CAP = CH * U + U
    NT = (SLOTS + E * (U - 1)) // U
    SKIP = LAST * U - START_LAST
    assert tuple(out.shape) == (N + U + SKIP, D)
    region_dram = nc.dram_tensor("expert_regions", [E * CAP + U, ROW], F32, kind="Internal").ap()

    with ExitStack() as ctx:
        def sb(name, shape, dt=F32):
            return ctx.enter_context(nc.sbuf_tensor(name, shape, dt))

        def sem(name):
            return ctx.enter_context(nc.semaphore(name))

        nat_at = -(-nc.sbuf_base // 32) * 32
        adjT_at = nat_at + NAT * HR * J * 4
        h_at = adjT_at + TS * KP * U * 4
        high_at = h_at + (KT + 1) * D * 4

        def placed(name, shape, at, dt=F32R):
            return nc.alloc_sbuf_tensor_at(name, shape, dt, offset=at)

        nat = sb("nat", [P, NAT, HR, J])
        adjT = sb("adjT", [P, TS, KP, U])
        h_rows = sb("h_rows", [P, KT + 1, D])
        h_high = sb("h_high", [P, PIECES, SPLIT, D], F32R)
        adj_high = sb("adj_high", [P, SPLIT, U], F32R)
        h_rest = placed("h_rest", [P, KT + 1, D], h_at)
        adj_rest = placed("adj_rest", [P, TS, KP, U], adjT_at)
        rem_nat = sb("rem_nat", [BLK, R, BLK])
        rem_T = sb("rem_T", [BLK, U])
        xin = sb("xin", [P, 2, U // P, D])
        xn1 = sb("xn1", [P, U // P, D])
        xnT = sb("xnT", [P, U])
        gT = sb("gT", [P, U])
        x1 = sb("x1", [P, 2, U // P, D])
        xn2 = sb("xn2", [P, U // P, D])
        rows = sb("rows", [P, 2, U // P, K, ROW])
        xn2T = sb("xn2T", [P, U])
        ident = sb("ident", [P, P])
        iota_e = sb("iota_e", [P, E])
        half_neg = sb("half_neg", [P, 4])
        base_e = sb("base_e", [P, 4])
        eps4 = sb("eps4", [P, 4])
        wiT = sb("wiT", [P, D])
        wuT = sb("wuT", [P, D])
        bi_rows = sb("bi_rows", [P, D])
        br_rows = sb("br_rows", [P, E])
        bu_col = sb("bu_col", [P, 1])
        wr_sb = sb("wr_sb", [P, E])
        moments = [sb(f"ln{n}_stats", [P, 4, 6]) for n in (1, 2, 3)]
        mean_var = [sb(f"ln{n}_mean_var", [P, 4, 2]) for n in (1, 2, 3)]
        var_eps = [sb(f"ln{n}_var_eps", [P, 4]) for n in (1, 2, 3)]
        rstds = [sb(f"ln{n}_rstd", [P, 4]) for n in (1, 2, 3)]
        logit = sb("logit", [P, 4, E])
        top = sb("top", [P, 4, 8])
        top_i = sb("top_i", [P, 4, 8], U32)
        top_f = sb("top_f", [P, 4, 2])
        gap = sb("gap", [P, 4])
        egap = sb("egap", [P, 4])
        esum = sb("esum", [P, 4])
        pick_w = sb("pick_w", [P, 4, 2])
        is_pick = sb("is_pick", [P, K, 4, E])
        mask = sb("mask", [P, 4, E], BF16)
        before_me = sb("before_me", [P, P], BF16)
        ones = sb("ones", [P, P], BF16)
        region_end = sb("region_end", [P, E])
        pos = sb("pos", [P, 4, E])
        pos_pick = sb("pos_pick", [P, K, 4, E])
        dest_f = sb("dest_f", [P, K, 4])
        dest = sb("dest", [P, 2, K * 4], U32)
        place_f = sb("place_f", [P, 4])
        place_last = sb("place_last", [P, 4])
        count = sb("count", [1, E])
        steps_512 = sb("steps_512", [1, CH + 1])
        n_tiles = sb("n_tiles", [1, E])
        upto = sb("upto", [1, E, E])
        upto_n = sb("upto_n", [1, E, E])
        last_tile = sb("last_tile", [1, E])
        tile_no = sb("tile_no", [1, NT])
        tab_past = sb("tab_past", [1, NT])
        tab_n = sb("tab_n", [1, NT])
        tab_rel = sb("tab_rel", [1, NT])
        tab_rowf = sb("tab_rowf", [1, NT])
        tab_row = sb("tab_row", [1, NT], U32)
        tab_e = sb("tab_e", [1, NT], U32)
        end_u = sb("end_u", [1, E], U32)
        place_now = sb("place_now", [P, 2, 4], U32)
        weight_now = sb("weight_now", [P, 2, 4])
        b1s = sb("b1s", [P, 2, HC])
        b2s = sb("b2s", [P, 2, 1])
        parT = sb("parT", [P, P])
        wi_nat, wu_nat, par = (adjT[:, 1, 2, n * P:(n + 1) * P] for n in range(3))
        featT = adjT[:, 1, 0:2, :]
        flat = nat[:, :, :, :].rearrange("p s r j -> p (s r j)")
        flat_T = adjT[:, :, :, :].rearrange("p s k u -> p (s k u)")
        EH = E * H
        w1_raw = flat[:, 0:EH].rearrange("p (e h) -> p e h", e=E)
        w2_raw = flat[:, EH:2 * EH].rearrange("p (e h) -> p e h", e=E)
        w1_all = placed("w1_all", [P, E, 2, H], h_at)
        x_lo = placed("x_lo", [P, 2, U], h_at + 2 * EH * 4)
        w2_all = placed("w2_all", [P, E, 2, H], adjT_at)
        h_hi = placed("h_hi", [P, 2, HC, U], adjT_at + 2 * EH * 4)
        yT = flat_T[:, 2 * EH + 2 * HC * U:2 * EH + 2 * HC * U + U]
        h_full = flat[:, 0:2 * HC * U].rearrange("p (s c u) -> p s c u", s=2, c=HC)
        h_lo = placed("h_lo", [P, 2, HC, U], nat_at)
        w1s = placed("w1s", [P, 2, 2, H], nat_at + 2 * EH * 4)
        w2s = placed("w2s", [P, 2, 2, H], nat_at + (2 * EH + 4 * H) * 4)
        x_hi = placed("x_hi", [P, 2, U], nat_at + (2 * EH + 8 * H) * 4)
        assert 2 * EH + 8 * H + 2 * U <= NAT * HR * J and 2 * EH + 2 * U <= (KT + 1) * D
        assert 2 * EH + 2 * HC * U + U <= TS * KP * U
        spare = placed("spare", [P, SPLIT * (PIECES * D + U)], high_at, F32)[:]
        y_rows = spare[:, 0:2 * U].rearrange("p (s t d) -> p s t d", s=2, d=D)
        xs = spare[:, 1024:1024 + 8 * ROW].rearrange("p (s t d) -> p s t d", s=2, t=4)
        over = spare[0:1, 2080:2080 + E * (CH + 1)].rearrange("p (e n) -> p e n", e=E)
        past = spare[0:1, 2400:2400 + NT * E].rearrange("p (n e) -> p n e", e=E)
        past_n = spare[0:1, 2800:2800 + NT * E].rearrange("p (n e) -> p n e", e=E)
        places = spare[:, 3200:3200 + NT * 8].rearrange("p (n t c) -> p n t c", t=4, c=2)
        fill = spare[:, 3600:3600 + 4 * ROW].rearrange("p (t r) -> p t r", r=ROW)
        cols = spare[:, 4160:4160 + E * (HC + 1)].rearrange("p (e c) -> p e c", e=E)

        bank = [ctx.enter_context(nc.psum_tensor(f"bank{n}", [P, 512], F32)) for n in range(8)]
        acc = bank[0:2]
        ps_x, ps_g, ps_n2, ps_n3, ps_l, ps_w = bank[2:8]

        consts_loaded = sem("consts_loaded")
        feat_loaded = [sem(f"feat_loaded{n}") for n in range(len(FEAT_PARTS))]
        first_loaded = sem("first_loaded")
        nat_loaded = [sem(f"nat_loaded{s}") for s in range(NAT)]
        rem_loaded = sem("rem_loaded")
        x_loaded = [sem(f"x_loaded{s}") for s in range(2)]
        passed = sem("passed")
        ident_zero = sem("ident_zero")
        par_zero = sem("par_zero")
        top_i_ready = sem("top_i_ready")
        ident_ready = sem("ident_ready")
        bases_ready = sem("bases_ready")
        wT_psum = sem("wT_psum")
        wT_ready = sem("wT_ready")
        feat_turned = sem("feat_turned")
        featT_ready = sem("featT_ready")
        h_psum = sem("h_psum")
        h_ready = sem("h_ready")
        h_zeroed = sem("h_zeroed")
        adj_turned = sem("adj_turned")
        h_high_ready = sem("h_high_ready")
        h_rest_ready = sem("h_rest_ready")
        adj_high_ready = sem("adj_high_ready")
        adj_rest_ready = sem("adj_rest_ready")
        rem_turned = sem("rem_turned")
        piece_used = sem("piece_used")
        acc_done = sem("acc_done")
        g_ready = sem("g_ready")
        g_turned = sem("g_turned")
        ln_st = [sem(f"ln{n}_st") for n in (1, 2, 3)]
        ln_mv = [sem(f"ln{n}_mv") for n in (1, 2, 3)]
        ln_ve = [sem(f"ln{n}_ve") for n in (1, 2, 3)]
        ln_rs = [sem(f"ln{n}_rs") for n in (1, 2, 3)]
        xn1_ready = sem("xn1_ready")
        xn1_turned = sem("xn1_turned")
        xnT_ready = sem("xnT_ready")
        x1_ready = sem("x1_ready")
        w_rows_ready = sem("w_rows_ready")
        masks_ready = sem("masks_ready")
        mask_ready = sem("mask_ready")
        ranks_psum = sem("ranks_psum")
        pos_steps = sem("pos_steps")
        dest_ready = sem("dest_ready")
        place_next = sem("place_next")
        scattered = [sem(f"scattered{s}") for s in range(2)]
        table_steps = sem("table_steps")
        table_ready = sem("table_ready")
        ends_ready = sem("ends_ready")
        filled = sem("filled")
        cols_ready = sem("cols_ready")
        xs_loaded = [sem(f"xs_loaded{s}") for s in range(2)]
        xs_turned = sem("xs_turned")
        x_hi_ready = sem("x_hi_ready")
        x_lo_ready = sem("x_lo_ready")
        places_ready = sem("places_ready")
        w1_ready = sem("w1_ready")
        w2_ready = sem("w2_ready")
        up_psum = sem("up_psum")
        gelu_ready = sem("gelu_ready")
        h_hi_ready = sem("h_hi_ready")
        h_lo_ready = sem("h_lo_ready")
        y_psum = sem("y_psum")
        yT_ready = sem("yT_ready")
        y_turned = sem("y_turned")
        y_rows_ready = sem("y_rows_ready")
        place_now_ready = sem("place_now_ready")
        weight_now_ready = sem("weight_now_ready")
        y_added = sem("y_added")
        rest_zeroed = sem("rest_zeroed")
        w_hi = sem("w_hi")
        w_split = sem("w_split")
        x1_stored = [sem(f"x1_stored{s}") for s in range(2)]
        xn2_ready = sem("xn2_ready")
        xn3_ready = sem("xn3_ready")
        xn2_turned = sem("xn2_turned")
        xn2T_ready = sem("xn2T_ready")
        logits_psum = sem("logits_psum")
        logits_ready = sem("logits_ready")
        top_ready = sem("top_ready")
        gap_ready = sem("gap_ready")
        egap_ready = sem("egap_ready")
        pick_steps = sem("pick_steps")
        w1_loaded = sem("w1_loaded")
        w2_loaded = sem("w2_loaded")
        par_turned = sem("par_turned")
        parT_ready = sem("parT_ready")
        b1_psum = sem("b1_psum")

        item_groups = [list(range(4 * q, min(4 * q + 4, KT))) for q in range(-(-KT // 4))]
        item_groups[-1].append(KT)
        NQ = len(item_groups)

        class At:

            def __init__(self, c, parity, before):
                self.c, self.s, self.before = c, parity, before
                self.fixed = isinstance(c, int)
                self.there = not self.fixed or 0 <= c <= LAST
                self.last = self.fixed and c == LAST

            def back(self, n):
                s = (self.s - n) % 2
                return At(self.c - n, s, self.before + (self.s - n - s) // 2)

            @property
            def n(self):
                return U_LAST if self.last else U

            def tiles(self):
                return [(t, t * P, min(P, self.n - t * P)) for t in range(-(-self.n // P))]

            def rows(self, a):
                return a[START_LAST:N, :] if self.last else self.span(a)

            def span(self, a):
                return a[self.c * U:self.c * U + U, :] if self.fixed else a[bass.ds(self.c * U, U), :]

            def own(self, a):
                return a[self.c, :, :] if self.fixed else a[bass.ds(self.c, 1), :, :].rearrange("a p n -> (a p) n")

        def chunks(eng, step, lo, lag, total=CH):
            hi = total - 2
            hi -= (hi - lo) % 2
            for c in range(lo):
                step(At(c, c % 2, c // 2))
            with eng.Fori(0, (hi - lo) // 2) as pair:
                for s in range(2):
                    step(At(pair * 2 + (lo + s), s, pair + lo // 2))
            for c in range(hi, total + lag):
                step(At(c, c % 2, c // 2))

        def after(eng, s, n):
            if not isinstance(n, int) or n > 0:
                eng.wait_ge(s, n)

        def wait_alone(eng, s, n):
            eng.wait_ge(s, n)
            eng.sem_inc(passed, 1)

        def halves(k, i):
            for n in (2 * i, 2 * i + 1):
                a = n % 2 * HR
                yield n % NAT, n + 1, n // NAT + 1, a, min(a + HR, k.n // BLK)

        def load_adj(eng, k, i, ranges):
            rows = k.rows(adj)
            for s, n, _, a, b in halves(k, i):
                after(eng, adj_turned, k.c * (2 * PIECES) + (n - NAT))
                for g in ranges:
                    eng.dma_start(nat[g * BLK:(g + 1) * BLK, s, 0:b - a, :],
                                  rows[a * BLK:b * BLK, g * GI + i * J:g * GI + (i + 1) * J]
                                  .rearrange("(r a) j -> a r j", a=BLK)).then_inc(nat_loaded[s], 16)

        def load_features(eng, ranges, parts):
            for n in parts:
                a, b = FEAT_PARTS[n]
                for g in ranges:
                    eng.dma_start(h_rows[g * BLK:(g + 1) * BLK, a:b, :],
                                  item_feat[g * GI + a * BLK:g * GI + b * BLK, :].rearrange("(k j) f -> j k f", j=BLK)
                                  ).then_inc(feat_loaded[n], 16)
            if NG - 1 in ranges and len(FEAT_PARTS) - 1 in parts:
                eng.dma_start(h_rows[0:BLK, KT, :], item_feat[REM0:N, :]).then_inc(feat_loaded[-1], 16)

        def turn(pe, dst, src, k):
            for t, t0, m in k.tiles():
                ins = pe.transpose(dst[:, t0:t0 + m], src[0:m, t, :], ident[0:m, 0:m])
            return ins

        def turn_back(pe, dst, src, k):
            for t, t0, m in k.tiles():
                ins = pe.transpose(dst[0:m, t * D:(t + 1) * D], src[:, t0:t0 + m], ident[:])
            return ins

        def move_rows(eng, k, dst_of, src_of, whole, s, per_chunk):
            if not k.last:
                eng.dma_start(*whole).then_inc(s, 16)
            else:
                for t, t0, m in k.tiles():
                    eng.dma_start(dst_of(t, t0, m), src_of(t, t0, m)).then_inc(s, 16)

        LT = len(At(LAST, 0, 0).tiles())

        def moved(k):
            return (k.before + (LT if k.last else 1)) * 16

        def scatters(k):
            return (k.before * 4 + len(k.tiles())) * (K * 16)

        def fill_up(eng, experts):
            for e in experts:
                end = eng.value_load(end_u[0:1, e:e + 1], min_val=e * CAP, max_val=(e + 1) * CAP - U)
                eng.dma_start(region_dram[bass.ds(end, U), :].rearrange("(t p) d -> p t d", p=P), fill
                              ).then_inc(filled, 16)

        block = ctx.enter_context(nc.Block())

        @block.sync
        def _(sp):
            for dst, src in [(wi_nat, W_item), (wu_nat, W_user),
                             (bi_rows[:], b_item.rearrange("(a d) -> a d", a=1).broadcast_to([P, D]))]:
                sp.dma_start(dst, src).then_inc(first_loaded, 16)
            load_features(sp, (0, 1), (0,))
            load_features(sp, range(NG), (1,))
            sp.wait_ge(par_zero, 1)
            small = [(br_rows[:], br.rearrange("(a d) -> a d", a=1).broadcast_to([P, E])),
                     (bu_col[:], b_user.rearrange("(d a) -> d a", a=1)), (wr_sb[:], Wr),
                     (par[0:E * HC, :], b1.rearrange("e (c p) -> (e c) p", p=P)),
                     (par[32:32 + E, :], ln_g), (par[64:64 + E, :], ln_b), (par[96:96 + E, :], b2)]
            assert len(small) == SMALL
            for dst, src in small:
                sp.dma_start(dst, src).then_inc(consts_loaded, 16)

            def step(k):
                k2 = k.back(2)
                if k.fixed and k.c == CH:
                    sp.wait_ge(adj_turned, CH * (2 * PIECES))
                    sp.dma_start(w1_raw, W1.rearrange("e d h -> d e h")).then_inc(w1_loaded, 16)
                    for e in range(E):
                        sp.dma_start(w2_raw[:, e, :].rearrange("p (c d) -> p c d", c=HC), W2[e, :, :].rearrange("(c p) d -> p c d", p=P)
                                     ).then_inc(w2_loaded, 16)
                for i in range(PIECES):
                    if k.there:
                        load_adj(sp, k, i, (0, 1))
                    if i == 1 and k.there:
                        after(sp, x1_ready, k.c - 1)
                        xr = k.rows(x)
                        move_rows(sp, k, lambda t, t0, m: xin[0:m, k.s, t, :], lambda t, t0, m: xr[t0:t0 + m, :],
                                  (xin[:, k.s, :, :], xr.rearrange("(t p) d -> p t d", p=P) if not k.last else None),
                                  x_loaded[k.s], 16)
                        after(sp, rem_turned, k.c)
                        sp.dma_start(rem_nat[:, 0:k.n // BLK, :],
                                     k.rows(adj)[:, REM0:N].rearrange("(r a) j -> a r j", a=BLK)
                                     ).then_inc(rem_loaded, 16)
                    if i == 2 and k2.there:
                        sp.wait_ge(x1_ready, k2.c + 1)
                        o = k2.rows(out[0:N, :])
                        move_rows(sp, k2, lambda t, t0, m: o[t0 + (0 if t else SKIP):t0 + m, :],
                                  lambda t, t0, m: x1[(0 if t else SKIP):m, k2.s, t, :],
                                  (o.rearrange("(t p) d -> p t d", p=P) if not k2.last else None, x1[:, k2.s, :, :]),
                                  x1_stored[k2.s], 16)

            chunks(sp, step, 6, 2)

            sp.wait_ge(masks_ready, 4)
            sp.dma_start(out[N:N + U, :].rearrange("(t p) d -> p t d", p=P), fill[:, :, 0:D]).then_inc(rest_zeroed, 16)
            sp.dma_start(out[N + U:N + U + SKIP, :], fill[0:SKIP, 0, 0:D]).then_inc(rest_zeroed, 16)
            sp.dma_start(region_dram[E * CAP:E * CAP + U, :].rearrange("(t p) d -> p t d", p=P), fill).then_inc(filled, 16)
            sp.wait_ge(ends_ready, 1)
            fill_up(sp, range(0, E, 2))
            for s in range(2):
                sp.wait_ge(x1_stored[s], moved(At(CH - 2 + s, s, CH // 2 - 1)))
                sp.wait_ge(scattered[s], scatters(At(CH - 2 + s, s, CH // 2 - 1)))
            sp.wait_ge(rest_zeroed, 32)
            sp.wait_ge(filled, 16 * (E + 1))
            sp.wait_ge(acc_done, CH)
            sp.wait_ge(table_ready, 1)

            def load_tile(k):
                if isinstance(k.c, int) and k.c >= NT:
                    return
                after(sp, xs_turned, k.c - 1)
                after(sp, places_ready, k.c - 1)
                start = sp.value_load(tab_row[0:1, k.c:k.c + 1] if k.fixed else tab_row[0:1, bass.ds(k.c, 1)],
                                      min_val=0, max_val=E * CAP)
                sp.dma_start(xs[:, k.s, :, :], region_dram[bass.ds(start, U), :].rearrange("(t p) d -> p t d", p=P)
                             ).then_inc(xs_loaded[k.s], 16)

            chunks(sp, load_tile, 2, 0, NT)

            sp.wait_ge(y_added, NT * 64)

        @block.scalar
        def _(act):
            load_features(act, (2, 3), (0,))
            act.wait_ge(wT_psum, 2)
            act.activation(wiT[:], ps_x[:, 0:D], ACT.Copy).then_inc(wT_ready, 1)
            act.activation(wuT[:], ps_x[:, D:2 * D], ACT.Copy).then_inc(wT_ready, 1)
            load_features(act, range(NG), (2,))
            load_adj(act, At(0, 0, 0), 0, (2, 3))
            for q in range(NQ):
                if q == 6:
                    load_adj(act, At(0, 0, 0), 1, (2, 3))
                act.wait_ge(feat_turned, q + 1)
                after(act, h_psum, q - 1)
                w = P * len(item_groups[q]) - (P - BLK) * (q == NQ - 1)
                act.activation(featT[:, q % 2, 0:w], bank[4 + q % 2][:, 0:w], ACT.Copy).then_inc(featT_ready, 1)
            act.wait_ge(par_turned, 1)
            act.activation(parT[:], ps_g[:, 0:P], ACT.Copy).then_inc(parT_ready, 1)
            act.wait_ge(h_ready, NQ + 1)
            for i in range(PIECES):
                act.activation(h_high[:, i, :, :], h_rows[:, i * KP + WHOLE:(i + 1) * KP, :], ACT.Copy
                               ).then_inc(h_high_ready, 1)

            def step(k):
                k1, k2, nxt = k.back(1), k.back(2), k.back(-1)
                for i in range(PIECES):
                    if i < PIECES - 2 and k.there:
                        load_adj(act, k, i + 2, (2, 3))
                    if i >= PIECES - 2 and nxt.there:
                        load_adj(act, nxt, i + 2 - PIECES, (2, 3))
                    if i == 0 and k1.there:
                        act.wait_ge(acc_done, k1.c + 1)
                        after(act, g_turned, k1.c)
                        act.activation(gT[:, 0:k1.n], acc[k1.s][:, 0:k1.n], ACT.Relu,
                                       bias=bu_col[:, 0:1]).then_inc(g_ready, 1)
                    if i == 0 and k2.there:
                        act.wait_ge(xn2_turned, k2.c + 1)
                        after(act, logits_psum, k2.c)
                        act.activation(xn2T[:, 0:k2.n], ps_n2[:, 0:k2.n], ACT.Copy).then_inc(xn2T_ready, 1)
                    if k.there:
                        act.wait_ge(adj_turned, k.c * (2 * PIECES) + (2 * i + 2))
                        after(act, piece_used, k.c * PIECES + i)
                        act.activation(adj_high[:, :, 0:k.n], adjT[:, i % TS, WHOLE:KP, 0:k.n], ACT.Copy
                                       ).then_inc(adj_high_ready, 1)
                    if i == 1 and k.there:
                        act.wait_ge(xn1_turned, k.c + 1)
                        after(act, acc_done, k.c)
                        act.activation(xnT[:, 0:k.n], ps_x[:, 0:k.n], ACT.Copy).then_inc(xnT_ready, 1)

            chunks(act, step, 6, 2)
            act.wait_ge(acc_done, CH)
            act.wait_ge(w2_loaded, 16 * E)
            act.activation(w2_all[:, :, 0, :], w2_raw, ACT.Copy
                           ).then_inc(w_hi, 1)
            act.wait_ge(w1_loaded, 16)
            for e in range(E):
                act.activation(w1_all[:, e, 0, :], w1_raw[:, e, :], ACT.Copy, scale=parT[:, 32 + e:33 + e]
                               ).then_inc(w_hi, 1)
            act.wait_ge(masks_ready, 4)
            act.wait_ge(ends_ready, 1)
            fill_up(act, range(1, E, 2))

            def x_high(k):
                act.wait_ge(xs_turned, k.c + 1)
                after(act, up_psum, (k.c - 1) * HC)
                act.activation(x_hi[:, k.s, :], bank[4][:], ACT.Copy).then_inc(x_hi_ready, 1)

            x_high(At(0, 0, 0))

            def tile(k):
                b, nxt = k.back(1), k.back(-1)
                if not k.fixed or k.c < NT:
                    after(act, y_psum, k.c - 1)
                    act.wait_ge(w1_ready, k.c + 1)
                    for m in range(HC):
                        act.wait_ge(up_psum, k.c * HC + (m + 1))
                        act.activation(h_full[:, k.s, m, :], bank[m][:], ACT.Gelu, bias=b1s[:, k.s, m:m + 1]
                                       ).then_inc(gelu_ready, 1)
                if not k.fixed or nxt.c < NT:
                    x_high(nxt)
                if not k.fixed or k.c < NT:
                    act.wait_ge(gelu_ready, (k.c + 1) * HC)
                    act.activation(h_hi[:, k.s, :, :], h_full[:, k.s, :, :], ACT.Copy
                                   ).then_inc(h_hi_ready, 1)
                if not k.fixed or b.c >= 0:
                    act.wait_ge(y_psum, b.c + 1)
                    after(act, y_turned, b.c)
                    act.activation(yT, bank[5][:], ACT.Identity, bias=b2s[:, b.s, 0:1]).then_inc(yT_ready, 1)

            chunks(act, tile, 4, 1, NT)

        @block.gpsimd
        def _(pool):
            pool.memset(ident[:], 0.0).then_inc(ident_zero, 1)
            pool.wait_ge(ident_zero, 1)
            pool.affine_select(out=ident[:], in_=ident[:], compare_op=ALU.not_equal, fill=1.0, base=0,
                               pattern=[[-1, P]], channel_multiplier=1).then_inc(ident_ready, 1)
            pool.memset(par, 0.0).then_inc(par_zero, 1)
            pool.iota(iota_e[:], [[1, E]], base=0, channel_multiplier=0,
                      allow_small_or_imprecise_dtypes=True).then_inc(bases_ready, 1)
            pool.memset(half_neg[:], -0.5).then_inc(bases_ready, 1)
            pool.memset(base_e[:], E_CONST).then_inc(bases_ready, 1)
            pool.memset(eps4[:], EPS).then_inc(bases_ready, 1)
            pool.memset(ones[:], 1.0).then_inc(masks_ready, 1)
            pool.wait_ge(masks_ready, 1)
            pool.affine_select(out=before_me[:], in_=ones[:], compare_op=ALU.is_gt, fill=0.0, base=0,
                               pattern=[[1, P]], channel_multiplier=-1).then_inc(masks_ready, 1)
            big = dict(channel_multiplier=0, allow_small_or_imprecise_dtypes=True)
            pool.iota(region_end[:], [[CAP, E]], base=0, **big).then_inc(bases_ready, 1)
            rising = dict(channel_multiplier=1, allow_small_or_imprecise_dtypes=True)
            pool.iota(place_f[:], [[P, 4]], base=0, **rising).then_inc(bases_ready, 1)
            pool.iota(place_last[:], [[P, 4]], base=START_LAST, **rising).then_inc(bases_ready, 1)
            pool.wait_ge(bases_ready, 7)
            pool.iota(place_last[0:SKIP, 0:1], [[1, 1]], base=N + U, **rising).then_inc(bases_ready, 1)
            pool.iota(steps_512[:], [[U, CH + 1]], base=0, **big).then_inc(bases_ready, 1)
            pool.iota(upto[:], [[1, E], [-1, E]], base=0, **big).then_inc(bases_ready, 1)
            pool.iota(tile_no[:], [[1, NT]], base=0, **big).then_inc(bases_ready, 1)
            pool.wait_ge(bases_ready, 11)

            def rstd(n, k):
                T = len(k.tiles())
                pool.wait_ge(ln_mv[n], k.c + 1)
                pool.tensor_tensor(var_eps[n][:, 0:T], mean_var[n][:, 0:T, 1], eps4[:, 0:T], ALU.add).then_inc(ln_ve[n], 1)
                pool.wait_ge(ln_ve[n], k.c + 1)
                pool.tensor_tensor(rstds[n][:, 0:T], var_eps[n][:, 0:T], half_neg[:, 0:T], ALU.pow).then_inc(ln_rs[n], 1)

            def adj_rests(k, i):
                if k.fixed and k.c == 0:
                    pool.wait_ge(h_high_ready, i + 1)
                    tiles = slice(i * KP + WHOLE, (i + 1) * KP)
                    pool.tensor_tensor(h_rest[:, tiles, :], h_rows[:, tiles, :], h_high[:, i, :, :].bitcast(F32),
                                       ALU.subtract).then_inc(h_rest_ready, 1)
                pool.wait_ge(adj_high_ready, k.c * PIECES + (i + 1))
                for j in range(SPLIT):
                    pool.tensor_tensor(adj_rest[:, i % TS, WHOLE + j, 0:k.n], adjT[:, i % TS, WHOLE + j, 0:k.n],
                                       adj_high[:, j, 0:k.n].bitcast(F32), ALU.subtract).then_inc(adj_rest_ready, 1)

            def dispatch(k, tiles, scatters=range(4 * K)):
                for t, t0, m in tiles:
                    for n in range(K):
                        if t * K + n not in scatters:
                            continue
                        pool.indirect_dma_start(
                            out=region_dram, out_offset=bass.IndirectOffsetOnAxis(
                                ap=dest[0:m, k.s, n * 4 + t:n * 4 + t + 1], axis=0),
                            in_=rows[0:m, k.s, t, n, :], in_offset=None).then_inc(scattered[k.s], 16)

            def dest_there(k):
                wait_alone(pool, w_rows_ready, k.c + 1)
                wait_alone(pool, dest_ready, k.c + 1)

            def second_weight(k):
                T = len(k.tiles())
                pool.wait_ge(gap_ready, k.c + 1)
                pool.tensor_tensor(egap[:, 0:T], base_e[:, 0:T], gap[:, 0:T], ALU.pow).then_inc(egap_ready, 1)

            def step(k):
                k1, k2, k3 = k.back(1), k.back(2), k.back(3)
                if k.fixed and k.c == CH:
                    pool.wait_ge(acc_done, CH)
                    pool.memset(fill, 0.0).then_inc(masks_ready, 1)
                    pool.wait_ge(masks_ready, 3)
                    pool.iota(fill[:, :, D].bitcast(U32), [[P, 4]], base=N, channel_multiplier=1
                              ).then_inc(masks_ready, 1)
                if k.fixed and k.c >= CH:
                    todo = k3.tiles()
                    dest_there(k3)
                    if k1.there:
                        dispatch(k3, todo[0:1])
                        rstd(1, k1)
                        dispatch(k3, todo[1:2])
                        second_weight(k2)
                        rstd(2, k1)
                        dispatch(k3, todo[2:])
                    elif k2.there:
                        second_weight(k2)
                        dispatch(k3, todo)
                    else:
                        dispatch(k3, todo)
                    return
                for i in range(PIECES):
                    if i == 0:
                        rstd(0, k)
                    if i == 3 and k1.there:
                        rstd(1, k1)
                    if i == 4 and k1.there:
                        rstd(2, k1)
                    if i == 4 and k2.there:
                        second_weight(k2)
                    adj_rests(k, i)
                    if i == 1 and k3.there:
                        dest_there(k3)
                    if i in (1, 2, 3) and k3.there:
                        dispatch(k3, k3.tiles(), range(3 * i - 3, min(3 * i, 4 * K)))

            chunks(pool, step, 6, 3)
            def tile(k):
                wait_alone(pool, places_ready, k.c + 1)
                if not k.fixed or k.c >= 2:
                    wait_alone(pool, y_rows_ready, k.c - 1)
                if not k.fixed or k.c >= 2:
                    wait_alone(pool, y_added, (k.c - 1) * 64)
                pl = places[:, k.c, :, :] if k.fixed else places[:, bass.ds(k.c, 1), :, :].rearrange("p a t c -> p (a t) c")
                pool.tensor_copy(place_now[:, k.s, :], pl[:, :, 0].bitcast(U32)).then_inc(place_now_ready, 1)
                pool.tensor_copy(weight_now[:, k.s, :], pl[:, :, 1]).then_inc(weight_now_ready, 1)
                wait_alone(pool, place_now_ready, k.c + 1)
                wait_alone(pool, y_rows_ready, k.c + 1)
                if not k.fixed or k.c >= 1:
                    wait_alone(pool, y_added, k.c * 64)
                for t in range(4):
                    pool.indirect_dma_start(
                        out=out, out_offset=bass.IndirectOffsetOnAxis(ap=place_now[:, k.s, t:t + 1], axis=0),
                        in_=y_rows[:, k.s, t, :], in_offset=None, compute_op=ALU.add).then_inc(y_added, 16)

            chunks(pool, tile, 2, 0, NT)

        @block.tensor
        def _(pe):
            pe.wait_ge(ident_ready, 1)
            pe.wait_ge(first_loaded, 16 * 3)
            pe.transpose(ps_x[:, 0:D], wi_nat, ident[:]).then_inc(wT_psum, 1)
            pe.transpose(ps_x[:, D:2 * D], wu_nat, ident[:]).then_inc(wT_psum, 1)

            pe.wait_ge(wT_ready, 2)
            for q in range(NQ + 1):
                if q == NQ:
                    pe.wait_ge(consts_loaded, 16 * SMALL)
                    pe.transpose(ps_g[:, 0:P], par, ident[:]).then_inc(par_turned, 1)
                if q < NQ:
                    for n, (a, b) in enumerate(FEAT_PARTS):
                        if a <= item_groups[q][0] < a + 4:
                            pe.wait_ge(feat_loaded[n], 16 * (NG + (n == len(FEAT_PARTS) - 1)))
                    after(pe, featT_ready, q - 1)
                    for n, t in enumerate(item_groups[q]):
                        m = BLK if t == KT else P
                        ins = pe.transpose(bank[4 + q % 2][:, n * P:n * P + m], h_rows[0:m, t, :], ident[0:m, 0:m])
                    ins.then_inc(feat_turned, 1)
                if q > 0:
                    b = q - 1
                    pe.wait_ge(featT_ready, b + 1)
                    after(pe, h_ready, b - 1)
                    for n, t in enumerate(item_groups[b]):
                        m = BLK if t == KT else P
                        ins = pe.matmul(bank[6 + b % 2][0:m, n * P:(n + 1) * P], featT[:, b % 2, n * P:n * P + m],
                                        wiT[:], start=True, stop=True)
                    ins.then_inc(h_psum, 1)
            pe.wait_ge(h_zeroed, 1)

            def step(k):
                k1, k2 = k.back(1), k.back(2)
                for i in range(PIECES):
                    if k.there:
                        if i == 0:
                            after(pe, g_ready, k.c - 1)
                        pe.wait_ge(adj_turned, k.c * (2 * PIECES) + (2 * i + 2))
                        for j in range(WHOLE):
                            pe.matmul(acc[k.s][:, 0:k.n], h_rows[:, i * KP + j, :], adjT[:, i % TS, j, 0:k.n],
                                      start=(i == 0 and j == 0), stop=False)
                        if k.fixed and k.c == 0:
                            pe.wait_ge(h_high_ready, PIECES)
                            pe.wait_ge(h_rest_ready, i + 1)
                        pe.wait_ge(adj_high_ready, k.c * PIECES + (i + 1))
                        for j in range(SPLIT):
                            at = i * KP + WHOLE + j
                            pe.matmul(acc[k.s][:, 0:k.n], h_high[:, i, j, :], adj_high[:, j, 0:k.n],
                                      start=False, stop=False)
                            pe.matmul(acc[k.s][:, 0:k.n], h_rest[:, at, :], adj_high[:, j, 0:k.n],
                                      start=False, stop=False)
                            pe.wait_ge(adj_rest_ready, k.c * (PIECES * SPLIT) + (i * SPLIT + j + 1))
                            ins = pe.matmul(acc[k.s][:, 0:k.n], h_high[:, i, j, :],
                                            adj_rest[:, i % TS, WHOLE + j, 0:k.n], start=False, stop=False)
                        ins.then_inc(piece_used, 1)
                    if i == 0 and k.there:
                        pe.wait_ge(xn1_ready, k.c + 1)
                        after(pe, xnT_ready, k.c)
                        turn(pe, ps_x, xn1, k).then_inc(xn1_turned, 1)
                    if i == 1 and k1.there:
                        pe.wait_ge(g_ready, k1.c + 1)
                        after(pe, x1_ready, k1.c)
                        turn_back(pe, ps_g, gT, k1).then_inc(g_turned, 1)
                    if i == 2 and k2.there:
                        pe.wait_ge(xn2T_ready, k2.c + 1)
                        after(pe, logits_ready, k2.c)
                        for t, t0, m in k2.tiles():
                            ins = pe.matmul(ps_l[0:m, t * E:(t + 1) * E], xn2T[:, t0:t0 + m], wr_sb[:],
                                            start=True, stop=True)
                        ins.then_inc(logits_psum, 1)
                    if i == 4 and k.there:
                        pe.wait_ge(xnT_ready, k.c + 1)
                        pe.matmul(acc[k.s][:, 0:k.n], wuT[:], xnT[:, 0:k.n], start=False, stop=False)
                    if i == 5 and k1.there:
                        pe.wait_ge(xn2_ready, k1.c + 1)
                        after(pe, xn2T_ready, k1.c)
                        turn(pe, ps_n2, xn2, k1).then_inc(xn2_turned, 1)
                    if i == 5 and k2.there:
                        pe.wait_ge(mask_ready, k2.c + 1)
                        after(pe, dest_ready, k2.c)
                        for t, t0, m in k2.tiles():
                            pe.matmul(ps_w[:, t * E:(t + 1) * E], before_me[0:m, :], mask[0:m, t, :],
                                      start=True, stop=(t == 0))
                            for b in range(t):
                                pe.matmul(ps_w[:, t * E:(t + 1) * E], ones[:], mask[:, b, :],
                                          start=False, stop=(b == t - 1))
                        for t, t0, m in k2.tiles():
                            ins = pe.matmul(ps_w[:, 4 * E:5 * E], ones[0:m, :], mask[0:m, t, :],
                                            start=(t == 0), stop=(m < P or t == 3))
                        ins.then_inc(ranks_psum, 1)
                if k.fixed and k.c == CH + 1:
                    pe.wait_ge(w1_loaded, 16)
                    for e in range(E):
                        for m in range(HC):
                            ins = pe.matmul(ps_x[:, e * HC + m:e * HC + m + 1], w1_raw[:, e, m * P:(m + 1) * P],
                                            parT[:, 64 + e:65 + e], start=True, stop=True)
                    ins.then_inc(b1_psum, 1)
                if k.there:
                    pe.wait_ge(rem_turned, k.c + 1)
                    pe.matmul(acc[k.s][:, 0:k.n], h_rows[0:BLK, KT, :], rem_T[:, 0:k.n],
                              start=False, stop=True).then_inc(acc_done, 1)

            chunks(pe, step, 6, 2)

            pe.wait_ge(g_ready, CH)
            pe.wait_ge(x1_ready, CH)
            pe.wait_ge(xn2T_ready, CH)
            pe.wait_ge(logits_ready, CH)
            whole = At(0, 0, 0)

            def turn_in(k):
                pe.wait_ge(xs_loaded[k.s], (k.before + 1) * 16)
                after(pe, x_lo_ready, k.c)
                turn(pe, bank[4], xs[:, k.s, :, 0:D], whole).then_inc(xs_turned, 1)

            def tile(k):
                b, bb, nxt = k.back(1), k.back(2), k.back(-1)
                if k.fixed and k.c == 0:
                    turn_in(k)
                if not k.fixed or k.c < NT:
                    pe.wait_ge(x_lo_ready, k.c + 1)
                    pe.wait_ge(x_hi_ready, k.c + 1)
                    pe.wait_ge(w1_ready, k.c + 1)
                    parts = [(0, x_hi), (0, x_lo), (1, x_hi)]
                    for m in range(HC):
                        after(pe, gelu_ready, k.c * HC + (m + 1 - HC))
                        for n, (w, xp) in enumerate(parts):
                            ins = pe.matmul(bank[m][:], w1s[:, k.s, w, m * P:(m + 1) * P],
                                            xp[:, k.s, :], start=(n == 0), stop=(n == 2))
                        ins.then_inc(up_psum, 1)
                if not k.fixed or nxt.c < NT:
                    turn_in(nxt)
                if not k.fixed or 0 <= b.c < NT:
                    pe.wait_ge(w2_ready, b.c + 1)
                    after(pe, yT_ready, b.c)
                    pe.wait_ge(h_hi_ready, b.c + 1)
                    pe.wait_ge(h_lo_ready, b.c + 1)
                    for m in range(HC):
                        for n, (w, hp) in enumerate([(0, h_hi), (1, h_hi), (0, h_lo)]):
                            ins = pe.matmul(bank[5][:], w2s[:, b.s, w, m * D:(m + 1) * D],
                                            hp[:, b.s, m, :],
                                            start=(m == 0 and n == 0), stop=(m == HC - 1 and n == 2))
                    ins.then_inc(y_psum, 1)
                if not k.fixed or 0 <= bb.c < NT:
                    pe.wait_ge(yT_ready, bb.c + 1)
                    after(pe, y_rows_ready, bb.c)
                    turn_back(pe, ps_l, yT, whole).then_inc(y_turned, 1)

            chunks(pe, tile, 4, 2, NT)

        @block.vector
        def _(dve):
            dve.wait_ge(first_loaded, 16 * 3)
            for q in range(NQ):
                dve.wait_ge(h_psum, q + 1)
                for n, t in enumerate(item_groups[q]):
                    if t == KT:
                        dve.tensor_tensor(h_rows[0:BLK, t, :], bank[6 + q % 2][0:BLK, n * P:(n + 1) * P],
                                          bi_rows[0:BLK, :], ALU.add).then_inc(h_ready, 1)
                full = [t for t in item_groups[q] if t < KT]
                w = len(full)
                ins = dve.tensor_tensor(h_rows[:, full[0]:full[0] + w, :],
                                        bank[6 + q % 2][:, 0:w * P].rearrange("p (k d) -> p k d", d=D),
                                        bi_rows[:].unsqueeze(1).to_broadcast([P, w, D]), ALU.add)
                ins.then_inc(h_ready, 1)
                if q >= NQ - KP:
                    j = q - (NQ - KP)
                    if j == 0:
                        dve.wait_ge(nat_loaded[0], 16 * NG)
                        dve.wait_ge(nat_loaded[1], 16 * NG)
                    ins = dve.transpose(adjT[:, 0, j, :], nat[:, 0:2, :, :].rearrange("p s r j -> p (s r) j")
                                        [:, :, j * BLK:(j + 1) * BLK])
            ins.then_inc(adj_turned, 2)
            dve.wait_ge(h_ready, NQ + 1)
            dve.memset(h_rows[0:REM_OLD, KT, :], 0.0).then_inc(h_zeroed, 1)

            def stats(n, src, k):
                after(dve, ln_rs[n], k.c)
                for t, t0, m in k.tiles():
                    ins = dve.bn_stats(moments[n][0:m, t, :], src[0:m, t, :])
                ins.then_inc(ln_st[n], 1)

            def aggregate(n, k):
                wait_alone(dve, ln_st[n], k.c + 1)
                for t, t0, m in k.tiles():
                    ins = dve.bn_aggr(mean_var[n][0:m, t, :], moments[n][0:m, t, :])
                ins.then_inc(ln_mv[n], 1)

            def normalise(n, dst, src, k, done):
                dve.wait_ge(ln_rs[n], k.c + 1)
                for t, t0, m in k.tiles():
                    ins = dve.tensor_scalar(dst[0:m, t, :], src[0:m, t, :], mean_var[n][0:m, t, 0:1], rstds[n][0:m, t:t + 1],
                                            ALU.subtract, ALU.mult)
                ins.then_inc(done, 1)

            def step(k):
                k1, k2, k3 = k.back(1), k.back(2), k.back(3)
                for i in range(PIECES):
                    if k.there and not (k.fixed and k.c == 0 and i == 0):
                        after(dve, piece_used, k.c * PIECES + (i - TS + 1))
                        for s, n, loads, a, b in halves(k, i):
                            dve.wait_ge(nat_loaded[s], (k.c * (2 * PIECES // NAT) + loads) * (16 * NG))
                            dve.transpose(adjT[:, i % TS, :, a * BLK:b * BLK].rearrange("p k (r a) -> p r k a", a=BLK),
                                          nat[:, s, 0:b - a, :].rearrange("p r (k j) -> p r k j", j=BLK)
                                          ).then_inc(adj_turned, 1)
                    if i == 0 and k.there:
                        xk = xin[:, k.s, :, :]
                        dve.wait_ge(x_loaded[k.s], moved(k))
                        stats(0, xk, k)
                        aggregate(0, k)
                    if i == 1 and k.there:
                        after(dve, xn1_turned, k.c)
                        normalise(0, xn1, xin[:, k.s, :, :], k, xn1_ready)
                    if i == 3 and k.there:
                        dve.wait_ge(rem_loaded, k.c * 16 + 16)
                        after(dve, acc_done, k.c)
                        dve.transpose(rem_T[:, 0:k.n], rem_nat[:, 0:k.n // BLK, :].rearrange("p r j -> p (r j)")
                                      ).then_inc(rem_turned, 1)
                    if i == 3 and k1.there:
                        dve.wait_ge(g_turned, k1.c + 1)
                        after(dve, x1_stored[k1.s], k1.before * 16)
                        for t, t0, m in k1.tiles():
                            ins = dve.tensor_tensor(x1[0:m, k1.s, t, :], ps_g[0:m, t * D:(t + 1) * D],
                                                    xin[0:m, k1.s, t, :], ALU.add)
                        ins.then_inc(x1_ready, 1)
                        dve.wait_ge(x1_ready, k1.c + 1)
                        stats(1, x1[:, k1.s, :, :], k1)
                        aggregate(1, k1)
                    if i == 1 and k3.there:
                        destinations(k3)
                    if i == 4 and k1.there:
                        after(dve, xn2_turned, k1.c)
                        normalise(1, xn2, x1[:, k1.s, :, :], k1, xn2_ready)
                        dve.wait_ge(xn2_ready, k1.c + 1)
                        stats(2, xn2, k1)
                        aggregate(2, k1)
                    if i == 4 and k2.there:
                        route_top(k2)
                    if i == 5:
                        if k1.there and not k1.last:
                            dispatch_rows(k1)
                        if k2.last:
                            dispatch_rows(k2)
                        if k2.there:
                            route_weights(k2)

            def dispatch_rows(k):
                after(dve, scattered[k.s], k.before * (4 * K * 16))
                dve.wait_ge(ln_rs[2], k.c + 1)
                for t, t0, m in k.tiles():
                    for n in range(K):
                        dve.tensor_scalar(rows[0:m, k.s, t, n, 0:D], xn2[0:m, t, :], mean_var[2][0:m, t, 0:1],
                                          rstds[2][0:m, t:t + 1], ALU.subtract, ALU.mult)
                after(dve, place_next, k.c)
                T = len(k.tiles())
                for n in range(K):
                    ins = dve.tensor_copy(rows[:, k.s, 0:T, n, D].bitcast(U32),
                                          (place_last if k.last else place_f)[:, 0:T])
                ins.then_inc(xn3_ready, 1)
                dve.wait_ge(xn3_ready, k.c + 1)
                dve.tensor_scalar(place_f[:], place_f[:], float(U), None, ALU.add).then_inc(place_next, 1)

            def route_top(k):
                T, c = len(k.tiles()), k.c
                dve.wait_ge(logits_psum, c + 1)
                for t, t0, m in k.tiles():
                    ins = dve.tensor_tensor(logit[0:m, t, :], ps_l[0:m, t * E:(t + 1) * E], br_rows[0:m, :], ALU.add)
                ins.then_inc(logits_ready, 1)
                wait_alone(dve, logits_ready, c + 1)
                for t, t0, m in k.tiles():
                    ins = dve.max(top[0:m, t, :], logit[0:m, t, :])
                ins.then_inc(top_ready, 1)
                wait_alone(dve, top_ready, c + 1)
                for t, t0, m in k.tiles():
                    ins = dve.max_index(top_i[0:m, t, :], top[0:m, t, :], logit[0:m, t, :])
                ins.then_inc(top_i_ready, 1)
                dve.wait_ge(top_i_ready, c + 1)
                dve.tensor_copy(top_f[:, 0:T, :], top_i[:, 0:T, 0:2])
                dve.tensor_tensor(gap[:, 0:T], top[:, 0:T, 1], top[:, 0:T, 0], ALU.subtract).then_inc(gap_ready, 1)

            def route_weights(k):
                T, c = len(k.tiles()), k.c
                dve.wait_ge(egap_ready, c + 1)
                dve.tensor_scalar(esum[:, 0:T], egap[:, 0:T], 1.0, None, ALU.add).then_inc(pick_steps, 1)
                after(dve, pos_steps, c * 4)
                for n in range(K):
                    for t in range(T):
                        ins = dve.tensor_scalar(is_pick[:, n, t, :], iota_e[:], top_f[:, t, n:n + 1], None, ALU.is_equal)
                ins.then_inc(pick_steps, 1)
                dve.wait_ge(pick_steps, c * 4 + 2)
                after(dve, w_rows_ready, c)
                dve.reciprocal(pick_w[:, 0:T, 0], esum[:, 0:T]).then_inc(pick_steps, 1)
                after(dve, ranks_psum, c)
                dve.tensor_tensor(mask[:, 0:T, :], is_pick[:, 0, 0:T, :], is_pick[:, 1, 0:T, :], ALU.add
                                  ).then_inc(mask_ready, 1)
                dve.wait_ge(pick_steps, c * 4 + 3)
                dve.tensor_tensor(pick_w[:, 0:T, 1], egap[:, 0:T], pick_w[:, 0:T, 0], ALU.mult).then_inc(pick_steps, 1)
                dve.wait_ge(pick_steps, c * 4 + 4)
                dve.tensor_copy(rows[:, k.s, 0:T, :, D + 1], pick_w[:, 0:T, :]).then_inc(w_rows_ready, 1)

            def destinations(k):
                T, c = len(k.tiles()), k.c
                dve.wait_ge(ranks_psum, c + 1)
                after(dve, pos_steps, c * 4)
                dve.tensor_tensor(pos[:, 0:T, :], ps_w[:, 0:T * E].rearrange("p (t e) -> p t e", e=E),
                                  region_end[:].unsqueeze(1).to_broadcast([P, T, E]), ALU.add).then_inc(pos_steps, 1)
                dve.wait_ge(pos_steps, c * 4 + 1)
                dve.tensor_tensor(region_end[:], ps_w[:, 4 * E:5 * E], region_end[:], ALU.add).then_inc(pos_steps, 1)
                for n in range(K):
                    ins = dve.tensor_tensor(pos_pick[:, n, 0:T, :], is_pick[:, n, 0:T, :], pos[:, 0:T, :], ALU.mult)
                ins.then_inc(pos_steps, 1)
                dve.wait_ge(pos_steps, c * 4 + 3)
                for n in range(K):
                    ins = dve.tensor_reduce(dest_f[:, n, 0:T], pos_pick[:, n, 0:T, :], AX.X, ALU.add)
                ins.then_inc(pos_steps, 1)
                dve.wait_ge(pos_steps, c * 4 + 4)
                after(dve, scattered[k.s], k.before * (4 * K * 16))
                for n in range(K):
                    ins = dve.tensor_copy(dest[:, k.s, n * 4:n * 4 + T], dest_f[:, n, 0:T])
                ins.then_inc(dest_ready, 1)

            chunks(dve, step, 6, 3)

            made = [0]

            def table(ins):
                made[0] += 1
                ins.then_inc(table_steps, 1)
                dve.wait_ge(table_steps, made[0])

            dve.wait_ge(pos_steps, CH * 4)
            dve.tensor_copy(end_u[:], region_end[0:1, :]).then_inc(ends_ready, 1)
            table(dve.tensor_scalar(count[:], iota_e[0:1, :], -float(CAP), None, ALU.mult))
            table(dve.tensor_tensor(count[:], region_end[0:1, :], count[:], ALU.add))
            table(dve.tensor_tensor(over, count[:].unsqueeze(2).to_broadcast([1, E, CH + 1]),
                                    steps_512[:].unsqueeze(1).to_broadcast([1, E, CH + 1]), ALU.is_gt))
            table(dve.tensor_reduce(n_tiles[:], over, AX.X, ALU.add))
            table(dve.tensor_scalar(upto[:], upto[:], 0.0, None, ALU.is_ge))
            table(dve.tensor_tensor(upto_n[:], upto[:], n_tiles[:].unsqueeze(1).to_broadcast([1, E, E]), ALU.mult))
            table(dve.tensor_reduce(last_tile[:], upto_n[:], AX.X, ALU.add))
            table(dve.tensor_tensor(past, tile_no[:].unsqueeze(2).to_broadcast([1, NT, E]),
                                    last_tile[:].unsqueeze(1).to_broadcast([1, NT, E]), ALU.is_ge))
            table(dve.tensor_tensor(past_n, past, n_tiles[:].unsqueeze(1).to_broadcast([1, NT, E]), ALU.mult))
            table(dve.tensor_reduce(tab_past[:], past, AX.X, ALU.add))
            table(dve.tensor_reduce(tab_n[:], past_n, AX.X, ALU.add))
            table(dve.tensor_tensor(tab_rel[:], tile_no[:], tab_n[:], ALU.subtract))
            table(dve.tensor_scalar(tab_rel[:], tab_rel[:], float(U), None, ALU.mult))
            table(dve.scalar_tensor_tensor(out=tab_rowf[:], in0=tab_past[:], scalar=float(CAP), in1=tab_rel[:],
                                           op0=ALU.mult, op1=ALU.add))
            table(dve.tensor_scalar(tab_rowf[:], tab_rowf[:], float(E * CAP), None, ALU.min))
            table(dve.tensor_scalar(tab_past[:], tab_past[:], float(E - 1), None, ALU.min))
            dve.tensor_copy(tab_row[:], tab_rowf[:])
            table(dve.tensor_copy(tab_e[:], tab_past[:]))
            dve.memset(count[:], 0.0).then_inc(table_ready, 1)

            dve.wait_ge(parT_ready, 1)
            dve.wait_ge(w_hi, 1)
            dve.tensor_tensor(w2_all[:, :, 1, :], w2_raw, w2_all[:, :, 0, :].bitcast(F32), ALU.subtract).then_inc(w_split, 1)
            for e in range(E):
                dve.wait_ge(w_hi, 2 + e)
                dve.scalar_tensor_tensor(out=w1_all[:, e, 1, :], in0=w1_raw[:, e, :],
                                         scalar=parT[:, 32 + e:33 + e], in1=w1_all[:, e, 0, :].bitcast(F32),
                                         op0=ALU.mult, op1=ALU.subtract).then_inc(w_split, 1)
            dve.wait_ge(b1_psum, 1)
            dve.tensor_tensor(cols[:, :, 0:HC], ps_x[:, 0:E * HC].rearrange("p (e c) -> p e c", e=E),
                              parT[:, 0:E * HC].rearrange("p (e c) -> p e c", e=E), ALU.add)
            dve.tensor_copy(cols[:, :, HC], parT[:, 96:96 + E]).then_inc(cols_ready, 1)
            dve.wait_ge(cols_ready, 1)
            dve.wait_ge(w_split, 1 + E)

            def expert_of(k):
                return dve.value_load(tab_e[0:1, k.c:k.c + 1] if k.fixed else tab_e[0:1, bass.ds(k.c, 1)],
                                      min_val=0, max_val=E - 1)

            def first_weights(k):
                if k.fixed and k.c >= NT:
                    return
                e = expert_of(k)
                if not k.fixed or k.c >= 2:
                    wait_alone(dve, up_psum, (k.c - 1) * HC)
                    wait_alone(dve, gelu_ready, (k.c - 1) * HC)
                w1f = w1_all[:].rearrange("p e x h -> p (e x h)")
                cf = cols.rearrange("p e c -> p (e c)")
                dve.tensor_copy(w1s[:, k.s, :, :].rearrange("p x h -> p (x h)"), w1f[:, bass.ds(e * (2 * H), 2 * H)])
                dve.tensor_copy(b1s[:, k.s, :], cf[:, bass.ds(e * (HC + 1), HC)]).then_inc(w1_ready, 1)

            def second_weights(k):
                if k.fixed and k.c >= NT:
                    return
                e = expert_of(k)
                if not k.fixed or k.c >= 2:
                    wait_alone(dve, yT_ready, k.c - 1)
                w2f = w2_all[:].rearrange("p e x h -> p (e x h)")
                cf = cols.rearrange("p e c -> p (e c)")
                dve.tensor_copy(b2s[:, k.s, :], cf[:, bass.ds(e * (HC + 1) + HC, 1)])
                dve.tensor_copy(w2s[:, k.s, :, :].rearrange("p x h -> p (x h)"), w2f[:, bass.ds(e * (2 * H), 2 * H)]
                                ).then_inc(w2_ready, 1)

            def rows_in(k):
                if k.fixed and k.c >= NT:
                    return
                dve.wait_ge(x_hi_ready, k.c + 1)
                dve.tensor_tensor(x_lo[:, k.s, :], bank[4][:], x_hi[:, k.s, :].bitcast(F32), ALU.subtract
                                  ).then_inc(x_lo_ready, 1)
                wait_alone(dve, xs_loaded[k.s], (k.before + 1) * 16)
                dve.tensor_copy((places[:, k.c, :, :] if k.fixed else
                                 places[:, bass.ds(k.c, 1), :, :].rearrange("p a t c -> p (a t) c")).bitcast(U32),
                                xs[:, k.s, :, D:D + 2].bitcast(U32)).then_inc(places_ready, 1)

            first_weights(At(0, 0, 0))
            rows_in(At(0, 0, 0))
            first_weights(At(1, 1, 0))
            second_weights(At(0, 0, 0))

            def tile(k):
                bb, nxt = k.back(2), k.back(-1)
                rows_in(nxt)
                first_weights(nxt.back(-1))
                if not k.fixed or k.c < NT:
                    dve.wait_ge(h_hi_ready, k.c + 1)
                    dve.tensor_tensor(h_lo[:, k.s, :, :], h_full[:, k.s, :, :], h_hi[:, k.s, :, :].bitcast(F32),
                                      ALU.subtract).then_inc(h_lo_ready, 1)
                second_weights(nxt)
                if not k.fixed or bb.c >= 0:
                    dve.wait_ge(y_turned, bb.c + 1)
                    dve.wait_ge(weight_now_ready, bb.c + 1)
                    after(dve, y_added, (bb.c - 1) * 64)
                    dve.tensor_tensor(y_rows[:, bb.s, :, :], ps_l[:].rearrange("p (t d) -> p t d", d=D),
                                      weight_now[:, bb.s, :].unsqueeze(2).to_broadcast([P, 4, D]), ALU.mult
                                      ).then_inc(y_rows_ready, 1)

            chunks(dve, tile, 4, 2, NT)


_INS = ['x', 'adj', 'L0_gnn_item_feat', 'L0_gnn_W_item', 'L0_gnn_b_item', 'L0_gnn_W_user', 'L0_gnn_b_user',
        'L0_ffn_Wr', 'L0_ffn_br', 'L0_ffn_ln_g', 'L0_ffn_ln_b', 'L0_ffn_W1', 'L0_ffn_b1', 'L0_ffn_W2', 'L0_ffn_b2']


def kernel(**inputs):
    import numpy as np
    from concourse import bacc
    from concourse.bass_utils import run_bass_kernel_spmd

    nc = bacc.Bacc("TRN2", target_bir_lowering=False, num_devices=1)
    arrays, args = {}, []
    for name in _INS:
        a = np.ascontiguousarray(inputs[name])
        arrays["in_" + name] = a
        args.append(nc.dram_tensor("in_" + name, a.shape, mybir.dt.from_np(a.dtype), kind="ExternalInput").ap())
    n, d = arrays["in_x"].shape
    res = nc.dram_tensor("out_rows", [n + 512 + 16, d], F32, kind="ExternalOutput").ap()
    graph_moe_kernel(nc, *args, res)
    r = run_bass_kernel_spmd(nc, [arrays], core_ids=[0])
    return r.results[0]["out_rows"][0:n]
```
